# Optimizing a Trainium2 kernel written in Bass

```python
import numpy as np
import jax
import jax.numpy as jnp

def _softmax(x, axis=-1):
    return jax.nn.softmax(x, axis=axis)

def _gelu(x):
    return jax.nn.gelu(x, approximate=True)

def _silu(x):
    return jax.nn.silu(x)

def _sigmoid(x):
    return jax.nn.sigmoid(x)

def _layernorm(x, axis=-1, eps=1e-05):
    m = jnp.mean(x, axis=axis, keepdims=True)
    v = jnp.var(x, axis=axis, keepdims=True)
    return (x - m) / jnp.sqrt(v + eps)

def _scatter_add(tgt, idx, src, axis=0):
    return tgt.at[idx].add(src)

def _segment_sum(src, seg, n):
    return jax.ops.segment_sum(src, seg, n)
kernel_name = 'mk_gnn_preln_d2_gnn_r32_e9fbed'

def setup_inputs(seed: int=0):
    np.random.seed(seed)
    _w = jnp.asarray

    def _rec_inputs():
        import jax
        import jax.numpy as jnp
        _gk = jax.random.key(seed)
        x = -0.0005121 + 1.001 * jax.random.normal(jax.random.fold_in(_gk, 1), (3125, 64), jnp.float32)
        src = jax.random.randint(jax.random.fold_in(_gk, 2), (100000,), 0, 3125, jnp.int32)
        dst = jnp.minimum((3125 * jax.random.uniform(jax.random.fold_in(_gk, 3), (100000,)) ** 2.0).astype(jnp.int32), 99999)
        _o = jnp.argsort(dst, stable=True)
        src = src[_o]
        dst = dst[_o]
        edge_weight = jax.random.uniform(jax.random.fold_in(_gk, 12), (100000,), jnp.float32, 0.0, 0.999998)
        return (x, src, dst, edge_weight)
    x, src, dst, edge_weight = _rec_inputs()

    def _L0_gnn_setup():
        import jax, jax.numpy as jnp
        import numpy as np
        N_NODES = 50000
        N_EDGES = 25000
        D_FEAT = 64
        HIDDEN = 128

        def _ebm(edge_input, t, W1, b1, Wt, bt, W2, b2):
            t_emb = jax.nn.silu(t[:, None] * Wt + bt)
            h = jax.nn.silu(edge_input @ W1 + t_emb + b1)
            return h @ W2 + b2
        key = jax.random.key(seed)
        ks = jax.random.split(key, 8)
        x = jax.random.normal(ks[0], (N_NODES, D_FEAT), dtype=jnp.float32)
        edge_index = jax.random.randint(ks[1], (2, N_EDGES), 0, N_NODES, dtype=jnp.int64)
        t = jax.random.uniform(ks[2], (N_EDGES,), dtype=jnp.float32)
        s1 = 1.0 / np.sqrt(2 * D_FEAT)
        s2 = 1.0 / np.sqrt(HIDDEN)
        W1 = jax.random.normal(ks[3], (2 * D_FEAT, HIDDEN), dtype=jnp.float32) * s1
        b1 = jnp.zeros((HIDDEN,), dtype=jnp.float32)
        Wt = jax.random.normal(ks[4], (1, HIDDEN), dtype=jnp.float32)
        bt = jnp.zeros((HIDDEN,), dtype=jnp.float32)
        W2 = jax.random.normal(ks[5], (HIDDEN, 2 * D_FEAT), dtype=jnp.float32) * s2
        b2 = jnp.zeros((2 * D_FEAT,), dtype=jnp.float32)
        return {'x': x, 'edge_index': edge_index, 't': t, 'W1': W1, 'b1': b1, 'Wt': Wt, 'bt': bt, 'W2': W2, 'b2': b2}
    _L0_gnn_all = _L0_gnn_setup()
    _L0_gnn_in = {k: v for k, v in _L0_gnn_all.items() if k in ('W1', 'b1', 'Wt', 'bt', 'W2', 'b2')}
    del _L0_gnn_all

    def _L1_gnn_setup():
        import jax, jax.numpy as jnp
        import numpy as np
        N_NODES = 50000
        N_EDGES = 25000
        IN_DIM = 64
        OUT_DIM = 64
        ALPHA = 0.2
        key = jax.random.key(seed)
        k1, k2, k3, k4 = jax.random.split(key, 4)
        x = jax.random.normal(k1, (N_NODES, IN_DIM), dtype=jnp.float32)
        edge_index = jax.random.randint(k2, (2, N_EDGES), 0, N_NODES, dtype=jnp.int64)
        W = jax.random.normal(k3, (OUT_DIM, IN_DIM), dtype=jnp.float32) * (1.0 / np.sqrt(IN_DIM))
        a = jax.random.normal(k4, (1, 2 * OUT_DIM), dtype=jnp.float32) * (1.0 / np.sqrt(2 * OUT_DIM))
        return {'x': x, 'edge_index': edge_index, 'W': W, 'a': a}
    _L1_gnn_all = _L1_gnn_setup()
    _L1_gnn_in = {k: v for k, v in _L1_gnn_all.items() if k in ('W', 'a')}
    del _L1_gnn_all
    return {'x': x, 'src': src, 'dst': dst, 'edge_weight': edge_weight, 'L0_gnn_W1': _L0_gnn_in['W1'], 'L0_gnn_b1': _L0_gnn_in['b1'], 'L0_gnn_Wt': _L0_gnn_in['Wt'], 'L0_gnn_bt': _L0_gnn_in['bt'], 'L0_gnn_W2': _L0_gnn_in['W2'], 'L0_gnn_b2': _L0_gnn_in['b2'], 'L1_gnn_W': _L1_gnn_in['W'], 'L1_gnn_a': _L1_gnn_in['a']}

def reference(x, src, dst, edge_weight, L0_gnn_W1, L0_gnn_b1, L0_gnn_Wt, L0_gnn_bt, L0_gnn_W2, L0_gnn_b2, L1_gnn_W, L1_gnn_a):
    import jax
    import jax.numpy as jnp

    def _L0_gnn_ref(x, edge_index, t, W1, b1, Wt, bt, W2, b2):
        import jax, jax.numpy as jnp
        import numpy as np
        N_NODES = 50000
        N_EDGES = 25000
        D_FEAT = 64
        HIDDEN = 128

        def _ebm(edge_input, t, W1, b1, Wt, bt, W2, b2):
            t_emb = jax.nn.silu(t[:, None] * Wt + bt)
            h = jax.nn.silu(edge_input @ W1 + t_emb + b1)
            return h @ W2 + b2
        row, col = (edge_index[0], edge_index[1])
        edge_input = jnp.concatenate([x[row], x[col]], axis=1)
        edge_output = _ebm(edge_input, t, W1, b1, Wt, bt, W2, b2)
        d = edge_output.shape[1] // 2
        src_update = edge_output[:, :d]
        tgt_update = edge_output[:, d:]
        update = jnp.concatenate([src_update, tgt_update], axis=0)
        idx = jnp.concatenate([row, col], axis=0)
        return jax.ops.segment_sum(update, idx, num_segments=x.shape[0])

    def _L1_gnn_ref(x, edge_index, W, a):
        import jax, jax.numpy as jnp
        import numpy as np
        N_NODES = 50000
        N_EDGES = 25000
        IN_DIM = 64
        OUT_DIM = 64
        ALPHA = 0.2
        num_nodes = x.shape[0]
        h = x @ W.T
        src, dst = (edge_index[0], edge_index[1])
        a_src = a[0, :OUT_DIM]
        a_dst = a[0, OUT_DIM:]
        e = jax.nn.leaky_relu(h[src] @ a_src + h[dst] @ a_dst, ALPHA)
        seg_max = jax.ops.segment_max(e, src, num_segments=num_nodes)
        exp_e = jnp.exp(e - seg_max[src])
        denom = jax.ops.segment_sum(exp_e, src, num_segments=num_nodes)
        attention = exp_e / denom[src]
        h_prime = jax.ops.segment_sum(attention[:, None] * h[src], dst, num_segments=num_nodes)
        return jax.nn.elu(h_prime)
    edge_index = jnp.stack([src, dst])
    h = jnp.maximum(_layernorm(x, axis=-1), 0.0)
    x = x + _L0_gnn_ref(h, edge_index, edge_weight, L0_gnn_W1, L0_gnn_b1, L0_gnn_Wt, L0_gnn_bt, L0_gnn_W2, L0_gnn_b2)
    h = jnp.maximum(_layernorm(x, axis=-1), 0.0)
    x = x + _L1_gnn_ref(h, edge_index, L1_gnn_W, L1_gnn_a)
    return x

_drawn_inputs = setup_inputs


def setup_inputs(seed=0):
    import zlib

    import numpy as np

    out = dict(_drawn_inputs(seed))
    spreads = {'L0_gnn_b1': (0.0, 0.1), 'L0_gnn_bt': (0.0, 0.1), 'L0_gnn_b2': (0.0, 0.1)}
    factors = {'L1_gnn_a': 8.0}
    for name, (base, spread) in spreads.items():
        noise = np.random.default_rng([zlib.crc32(name.encode()), seed]).standard_normal(out[name].shape)
        drawn = base * np.exp(spread * noise) if base else spread * noise
        out[name] = jnp.asarray(drawn.astype(out[name].dtype))
    for name, factor in factors.items():
        out[name] = (out[name] * factor).astype(out[name].dtype)
    return out
```

```python
from contextlib import ExitStack

import numpy as np

import concourse.bass as bass
from concourse import mybir

P = 128
F32 = mybir.dt.float32
I32 = mybir.dt.int32
ALU = mybir.AluOpType
ACT = mybir.ActivationFunctionType
AX_X = mybir.AxisListType.X
EPS = 1e-5
SLOPE = 0.2
FAR = 1e30
BANK = 512


def build(nc, x, src, dst, edge_weight, W1, b1, Wt, bt, W2, b2, W, a, identity, below, spare, out):
    N, D = x.shape
    E = src.shape[0]
    H = W1.shape[1]
    NT = (N + P - 1) // P
    REST = N - (NT - 1) * P
    EP = max(k for k in range(1, P + 1) if E % k == 0)
    ET = E // EP
    U = 4
    G = ET // U
    R = G // 2
    W_ROW = H + 1
    assert ET == U * G and G == 2 * R and U * H == BANK and U * EP <= BANK and R >= 3 and 2 * D == H

    acc_src = nc.dram_tensor("acc_src", (N + EP, W_ROW), F32, kind="Internal").ap()
    acc_dst = nc.dram_tensor("acc_dst", (N + EP, W_ROW), F32, kind="Internal").ap()
    pairs = nc.dram_tensor("pairs", (N * N + EP, 1), F32, kind="Internal").ap()
    table_p = nc.dram_tensor("table_p", (N, H), F32, kind="Internal").ap()
    table_q = nc.dram_tensor("table_q", (N, H), F32, kind="Internal").ap()

    def rows(t):
        return P if t < NT - 1 else REST

    with ExitStack() as ctx:
        def sb(name, shape, dt=F32):
            return ctx.enter_context(nc.sbuf_tensor(name, shape, dt))

        def sem(name):
            return ctx.enter_context(nc.semaphore(name))

        ident = sb("ident", [P, P])
        x_sb = sb("x_sb", [P, NT, D])
        w2_sb = sb("w2_sb", [H, 2 * D])
        b2_row = sb("b2_row", [P, 2 * D])
        w_sb = sb("w_sb", [D, D])
        a_row = sb("a_row", [P, 2 * D])
        stats = sb("stats", [P, NT, 6])
        mean_var = sb("mean_var", [P, NT, 2])
        std = sb("std", [P, NT, 1])
        rstd = sb("rstd", [P, NT, 1])
        h_sb = sb("h_sb", [P, NT, D])
        psum = [ctx.enter_context(nc.psum_tensor(f"ps{i}", [P, BANK], F32)) for i in range(8)]

        loaded = sem("loaded")
        dve_step = sem("dve_step")
        zeros_set = sem("zeros_set")
        tail_set = sem("tail_set")
        zeroed = sem("zeroed")
        std_ready = sem("std_ready")
        var_ready = sem("var_ready")
        h_ready = sem("h_ready")
        hT_ready = sem("hT_ready")
        hT_used = sem("hT_used")
        pq_ready = sem("pq_ready")
        pq_copied = sem("pq_copied")
        stored = [sem("stored_0"), sem("stored_1")]

        class Chain:

            def __init__(self):
                self.n = 0

            def __call__(self, eng, ins):
                self.n += 1
                ins.then_inc(dve_step, 1)
                eng.wait_ge(dve_step, self.n)

        chain = Chain()

        def layer_norm(dve, step, rows_in, which):
            for t in range(NT):
                last = dve.bn_stats(stats[:, t, :], rows_in[:, t, :])
            step(dve, last)
            for t in range(NT):
                last = dve.bn_aggr(mean_var[:, t, :], stats[:, t, :])
            step(dve, last)
            dve.tensor_scalar(mean_var[:, :, 1:2], mean_var[:, :, 1:2], EPS, None,
                              ALU.add).then_inc(var_ready, 1)
            dve.wait_ge(std_ready, 1 + which)
            step(dve, dve.reciprocal(rstd[:, :, :], std[:, :, :]))
            step(dve, dve.tensor_tensor(h_sb[:, :, :], rows_in[:, :, :],
                                        mean_var[:, :, 0:1].to_broadcast([P, NT, D]), ALU.subtract))
            step(dve, dve.tensor_tensor(h_sb[:, :, :], h_sb[:, :, :],
                                        rstd[:, :, :].to_broadcast([P, NT, D]), ALU.mult))
            dve.tensor_scalar(h_sb[:, :, :], h_sb[:, :, :], 0.0, None, ALU.max).then_inc(h_ready, 1)

        with ExitStack() as early:
            def esb(name, shape, dt=F32):
                return early.enter_context(nc.sbuf_tensor(name, shape, dt))

            zeros = esb("zeros", [P, N])
            w1a = esb("w1a", [D + 1, H])
            w1b = esb("w1b", [D, H])
            hT = esb("hT", [D + 1, NT, P])
            pq = esb("pq", [P, 2, 2, H])

            with nc.Block() as block:
                def copy_pq(dve, t):
                    dve.wait_ge(pq_ready, t + 1)
                    if t >= 2:
                        dve.wait_ge(stored[t % 2], 32 * (t // 2))
                    dve.tensor_copy(pq[:, t % 2, :, :].rearrange("p a h -> p (a h)"),
                                    psum[2 + t % 2][:, 0:2 * H]).then_inc(pq_copied, 1)

                @block.sync
                def _(sp):
                    full = (NT - 1) * P
                    sp.wait_ge(tail_set, 1)
                    loads = [
                        (x_sb[:, 0:NT - 1, :], x[0:full, :].rearrange("(t p) d -> p t d", p=P)),
                        (x_sb[0:REST, NT - 1, :], x[full:N, :]),
                        (ident[:, :], identity),
                        (w1a[0:D, :], W1[0:D, :]),
                        (w1a[D:D + 1, :], b1.rearrange("(o n) -> o n", o=1)),
                        (w1b[:, :], W1[D:2 * D, :]),
                        (w2_sb[:, :], W2),
                        (b2_row[:, :], b2.rearrange("(o n) -> o n", o=1).to_broadcast([P, 2 * D])),
                        (w_sb[:, :], W),
                        (a_row[:, :], a.to_broadcast([P, 2 * D])),
                    ]
                    for to, of in loads:
                        sp.dma_start(to, of).then_inc(loaded, 16)
                    assert len(loads) == 10
                    for t in range(NT):
                        n = rows(t)
                        sp.wait_ge(pq_copied, t + 1)
                        sp.dma_start(table_p[t * P:t * P + n, :], pq[0:n, t % 2, 0, :]).then_inc(stored[t % 2], 16)
                        sp.dma_start(table_q[t * P:t * P + n, :], pq[0:n, t % 2, 1, :]).then_inc(stored[t % 2], 16)
                    sp.wait_ge(stored[0], 32 * ((NT + 1) // 2))
                    sp.wait_ge(stored[1], 32 * (NT // 2))

                @block.gpsimd
                def _(pool):
                    pool.memset(zeros[:, :], 0.0).then_inc(zeros_set, 1)

                @block.scalar
                def _(act):
                    act.wait_ge(zeros_set, 1)
                    n = 0
                    for k in range(N // EP):
                        act.dma_start(pairs[k * EP * N:(k + 1) * EP * N, :].rearrange("(p c) o -> p (c o)", p=EP),
                                      zeros[0:EP, :]).then_inc(zeroed, 16)
                        n += 1
                    for acc in (acc_src, acc_dst):
                        for k in range((N + EP) // EP):
                            act.dma_start(acc[k * EP:(k + 1) * EP, :], zeros[0:EP, 0:W_ROW]).then_inc(zeroed, 16)
                            n += 1
                    act.dma_start(pairs[N * N:N * N + EP, :], zeros[0:EP, 0:1]).then_inc(zeroed, 16)
                    n += 1
                    act.wait_ge(var_ready, 1)
                    nc.scalar.activation(std[:, :, :], mean_var[:, :, 1:2], ACT.Sqrt).then_inc(std_ready, 1)
                    act.wait_ge(zeroed, 16 * n)

                @block.vector
                def _(dve):
                    dve.memset(x_sb[:, NT - 1, :], 0.0).then_inc(tail_set, 1)
                    dve.memset(hT[D:D + 1, :, :], 1.0)
                    dve.wait_ge(loaded, 160)
                    layer_norm(dve, chain, x_sb, 0)
                    for t in range(NT):
                        dve.wait_ge(hT_ready, t + 1)
                        dve.tensor_copy(hT[0:D, t, :], psum[t % 2][0:D, 0:P]).then_inc(hT_used, 1)
                        if t >= 1:
                            copy_pq(dve, t - 1)
                    copy_pq(dve, NT - 1)

                @block.tensor
                def _(pe):
                    pe.wait_ge(loaded, 160)
                    pe.wait_ge(h_ready, 1)
                    for t in range(NT + 1):
                        if t < NT:
                            if t >= 2:
                                pe.wait_ge(hT_used, t - 1)
                            pe.transpose(psum[t % 2][0:D, 0:P], h_sb[:, t, :], ident[:, :]).then_inc(hT_ready, 1)
                        if t >= 1:
                            u = t - 1
                            pe.wait_ge(hT_used, u + 1)
                            if u >= 2:
                                pe.wait_ge(pq_copied, u - 1)
                            pe.matmul(psum[2 + u % 2][:, 0:H], hT[:, u, :], w1a[:, :], start=True, stop=True)
                            pe.matmul(psum[2 + u % 2][:, H:2 * H], hT[0:D, u, :], w1b[:, :],
                                      start=True, stop=True).then_inc(pq_ready, 1)

        with ExitStack() as mid:
            def msb(name, shape, dt=F32):
                return mid.enter_context(nc.sbuf_tensor(name, shape, dt))

            src_all = msb("src_all", [EP, ET], I32)
            dst_all = msb("dst_all", [EP, ET], I32)
            t_all = msb("t_all", [EP, ET])
            wt_row = msb("wt_row", [EP, H])
            bt_row = msb("bt_row", [EP, H])
            lower = msb("lower", [EP, EP])
            spare_sb = msb("spare_sb", [EP, 3])
            key_i = msb("key_i", [EP, 2, 2, U], I32)
            key_f = msb("key_f", [EP, 2, 3, U])
            temb = msb("temb", [EP, 2, U, H])
            t_now = msb("t_now", [EP, 2, U])
            rows_p = msb("rows_p", [EP, 2, U, H])
            rows_q = msb("rows_q", [EP, 2, U, H])
            equal = msb("equal", [EP, 2, 6, U, EP])
            counts = msb("counts", [EP, 2, 6, U])
            move = msb("move", [EP, 2, 3, U])
            to_row = msb("to_row", [EP, 2, 3, U], I32)
            hid = msb("hid", [EP, 2, U, H])
            sums = msb("sums", [EP, 2, 2, U, W_ROW])
            counted = msb("counted", [EP, 2, U])

            edges_loaded = sem("edges_loaded")
            keys_ready = sem("keys_ready")
            temb_in = sem("temb_in")
            temb_out = sem("temb_out")
            keys_turned = sem("keys_turned")
            equal_ready = sem("equal_ready")
            rows_ready = sem("rows_ready")
            pre_ready = sem("pre_ready")
            hid_ready = sem("hid_ready")
            summed = sem("summed")
            sums_ready = sem("sums_ready")
            fetched = [sem("fetched_0"), sem("fetched_1")]
            added_src = sem("added_src")
            added_dst = sem("added_dst")
            added_pair = sem("added_pair")
            pool_passed = sem("pool_passed")
            key_step = sem("key_step")
            pre_step = sem("pre_step")
            KEY_STEPS = 7

            def rounds(eng, work):
                work(0)
                with eng.Fori(1, R - 1) as r:
                    work(r)
                work(R - 1)

            def known(r, n):
                return isinstance(r, int) and r == n

            with nc.Block() as block:
                @block.sync
                def _(sp):
                    for to, of in (
                        (src_all[:, :], src.rearrange("(p i) -> p i", p=EP)),
                        (dst_all[:, :], dst.rearrange("(p i) -> p i", p=EP)),
                        (t_all[:, :], edge_weight.rearrange("(p i) -> p i", p=EP)),
                        (wt_row[:, :], Wt.to_broadcast([EP, H])),
                        (bt_row[:, :], bt.rearrange("(o n) -> o n", o=1).to_broadcast([EP, H])),
                        (lower[:, :], below),
                        (spare_sb[:, :], spare),
                    ):
                        sp.dma_start(to, of).then_inc(edges_loaded, 16)

                @block.gpsimd
                def _(pool):
                    def apart(pool):
                        pool.sem_inc(pool_passed, 1)

                    def fetch(r, q):
                        g = r * 2 + q
                        pool.wait_ge(keys_ready, g + 1)
                        if not known(r, 0):
                            pool.wait_ge(hid_ready, g - 1)
                        apart(pool)
                        for u in range(U):
                            for k, table, to in ((0, table_p, rows_p), (1, table_q, rows_q)):
                                pool.indirect_dma_start(
                                    to[:, q, u, :], None, table,
                                    bass.IndirectOffsetOnAxis(ap=key_i[:, q, k, u:u + 1], axis=0),
                                ).then_inc(fetched[q], 16)

                    def add(r, q):
                        g = r * 2 + q
                        pool.wait_ge(rows_ready, g + 1)
                        pool.wait_ge(sums_ready, g + 1)
                        for u in range(U):
                            for k, (onto, rows_in, done) in enumerate((
                                (acc_src, sums[:, q, 0, u, :], added_src),
                                (acc_dst, sums[:, q, 1, u, :], added_dst),
                                (pairs, counted[:, q, u:u + 1], added_pair),
                            )):
                                if not (known(r, 0) and q == u == 0):
                                    pool.wait_ge(done, (g * U + u) * 16)
                                    apart(pool)
                                pool.indirect_dma_start(
                                    onto, bass.IndirectOffsetOnAxis(ap=to_row[:, q, k, u:u + 1], axis=0),
                                    rows_in, None, compute_op=ALU.add,
                                ).then_inc(done, 16)

                    fetch(0, 0)

                    def work(r):
                        fetch(r, 1)
                        add(r, 0)
                        if not known(r, R - 1):
                            fetch(r + 1, 0)
                        add(r, 1)

                    rounds(pool, work)
                    for done in (added_src, added_dst, added_pair):
                        pool.wait_ge(done, 16 * ET)

                @block.vector
                def _(dve):
                    dve.wait_ge(edges_loaded, 7 * 16)

                    def keys(r, q):
                        g = r * 2 + q

                        def step(k, ins):
                            ins.then_inc(key_step, 1)
                            dve.wait_ge(key_step, g * KEY_STEPS + k)

                        cols = bass.ds(r * (2 * U) + q * U, U)
                        if not (isinstance(r, int) and r == 0):
                            for done in (added_src, added_dst, added_pair):
                                dve.wait_ge(done, (g - 1) * (U * 16))
                            dve.wait_ge(summed, g - 1)
                        dve.tensor_copy(key_i[:, q, 0, :], src_all[:, cols])
                        dve.tensor_copy(key_i[:, q, 1, :], dst_all[:, cols])
                        step(1, dve.tensor_copy(t_now[:, q, :], t_all[:, cols]))
                        dve.tensor_copy(key_f[:, q, 0:2, :], key_i[:, q, :, :]).then_inc(keys_ready, 1)
                        for u in range(U):
                            last = dve.scalar_tensor_tensor(temb[:, q, u, :], wt_row[:, :], t_now[:, q, u:u + 1],
                                                            bt_row[:, :], ALU.mult, ALU.add)
                        last.then_inc(temb_in, 1)
                        dve.wait_ge(temb_in, g + 1)
                        step(2, dve.scalar_tensor_tensor(key_f[:, q, 2, :], key_f[:, q, 0, :], float(N),
                                                         key_f[:, q, 1, :], ALU.mult, ALU.add))
                        dve.tensor_tensor(move[:, q, :, :], spare_sb[:, :].unsqueeze(2).to_broadcast([EP, 3, U]),
                                          key_f[:, q, :, :], ALU.subtract)
                        dve.wait_ge(keys_turned, g + 1)
                        for k in range(2):
                            last = dve.tensor_tensor(
                                equal[:, q, k, :, :],
                                psum[2 * k + q][0:EP, 0:U * EP].rearrange("p (u e) -> p u e", u=U),
                                key_f[:, q, k, :].unsqueeze(2).to_broadcast([EP, U, EP]), ALU.is_equal)
                        last.then_inc(equal_ready, 1)
                        dve.wait_ge(equal_ready, g + 1)
                        dve.tensor_tensor(equal[:, q, 2, :, :], equal[:, q, 0, :, :], equal[:, q, 1, :, :], ALU.mult)
                        step(3, dve.tensor_tensor(
                            equal[:, q, 3:5, :, :].rearrange("p k u e -> p (k u) e"),
                            equal[:, q, 0:2, :, :].rearrange("p k u e -> p (k u) e"),
                            lower[:, :].unsqueeze(1).to_broadcast([EP, 2 * U, EP]), ALU.mult))
                        step(4, dve.tensor_tensor(equal[:, q, 5, :, :], equal[:, q, 3, :, :], equal[:, q, 1, :, :],
                                                  ALU.mult))
                        step(5, dve.tensor_reduce(counts[:, q, :, :].rearrange("p k u -> p (k u)"),
                                                  equal[:, q, :, :, :].rearrange("p k u e -> p (k u) e"),
                                                  AX_X, ALU.add))
                        step(6, dve.scalar_tensor_tensor(move[:, q, :, :], counts[:, q, 3:6, :], 0.5,
                                                         move[:, q, :, :], ALU.is_gt, ALU.mult))
                        dve.tensor_tensor(to_row[:, q, :, :], move[:, q, :, :], key_f[:, q, :, :], ALU.add)
                        dve.tensor_copy(sums[:, q, :, :, H], counts[:, q, 0:2, :])
                        step(7, dve.tensor_copy(counted[:, q, :], counts[:, q, 2, :]))
                        dve.sem_inc(rows_ready, 1)

                    def before_silu(r, q):
                        g = r * 2 + q
                        dve.wait_ge(fetched[q], (r + 1) * (2 * U * 16))
                        dve.tensor_tensor(rows_p[:, q, :, :], rows_p[:, q, :, :], rows_q[:, q, :, :],
                                          ALU.add).then_inc(pre_step, 1)
                        dve.wait_ge(pre_step, g + 1)
                        dve.wait_ge(temb_out, g + 1)
                        dve.tensor_tensor(rows_p[:, q, :, :], rows_p[:, q, :, :], temb[:, q, :, :],
                                          ALU.add).then_inc(pre_ready, 1)

                    keys(0, 0)

                    def work(r):
                        keys(r, 1)
                        before_silu(r, 0)
                        if not known(r, R - 1):
                            keys(r + 1, 0)
                        before_silu(r, 1)

                    rounds(dve, work)

                @block.scalar
                def _(act):
                    def silu_time(r, q):
                        g = r * 2 + q
                        act.wait_ge(temb_in, g + 1)
                        nc.scalar.activation(temb[:, q, :, :], temb[:, q, :, :], ACT.Silu).then_inc(temb_out, 1)

                    def silu_hidden(r, q):
                        g = r * 2 + q
                        act.wait_ge(pre_ready, g + 1)
                        if not known(r, 0):
                            act.wait_ge(summed, g - 1)
                        nc.scalar.activation(hid[:, q, :, :], rows_p[:, q, :, :], ACT.Silu).then_inc(hid_ready, 1)

                    def take_sums(r, q):
                        g = r * 2 + q
                        act.wait_ge(summed, g + 1)
                        if not known(r, 0):
                            act.wait_ge(added_src, (g - 1) * (U * 16))
                            act.wait_ge(added_dst, (g - 1) * (U * 16))
                        for k in range(2):
                            last = nc.scalar.copy(sums[:, q, k, :, 0:H],
                                                  psum[4 + 2 * k + q][0:EP, :].rearrange("p (u h) -> p u h", u=U))
                        last.then_inc(sums_ready, 1)

                    silu_time(0, 0)

                    def work(r):
                        silu_time(r, 1)
                        silu_hidden(r, 0)
                        take_sums(r, 0)
                        if not known(r, R - 1):
                            silu_time(r + 1, 0)
                        silu_hidden(r, 1)
                        take_sums(r, 1)

                    rounds(act, work)

                @block.tensor
                def _(pe):
                    def turn_keys(r, q):
                        g = r * 2 + q
                        pe.wait_ge(keys_ready, g + 1)
                        for k in range(2):
                            for u in range(U):
                                last = pe.transpose(psum[2 * k + q][0:EP, u * EP:(u + 1) * EP],
                                                    key_f[:, q, k, u:u + 1].to_broadcast([EP, EP]),
                                                    ident[0:EP, 0:EP])
                        last.then_inc(keys_turned, 1)

                    def sum_equal(r, q):
                        g = r * 2 + q
                        pe.wait_ge(equal_ready, g + 1)
                        pe.wait_ge(hid_ready, g + 1)
                        if not known(r, 0):
                            pe.wait_ge(sums_ready, g - 1)
                        for k in range(2):
                            for u in range(U):
                                last = pe.matmul(psum[4 + 2 * k + q][0:EP, u * H:(u + 1) * H],
                                                 equal[:, q, k, u, :], hid[:, q, u, :], start=True, stop=True)
                        last.then_inc(summed, 1)

                    turn_keys(0, 0)

                    def work(r):
                        turn_keys(r, 1)
                        sum_equal(r, 0)
                        if not known(r, R - 1):
                            turn_keys(r + 1, 0)
                        sum_equal(r, 1)

                    rounds(pe, work)

        x1 = sb("x1", [P, NT, D])
        hh = sb("hh", [P, NT, D])
        from_src = sb("from_src", [P, NT])
        nodes_summed = sem("nodes_summed")
        sT_ready = sem("sT_ready")
        sT_used = sem("sT_used")
        up_ready = sem("up_ready")
        up_used = sem("up_used")
        NP = NT * P
        CH = [(c, min(BANK, NP - c)) for c in range(0, NP, BANK)]
        late = ctx.enter_context(ExitStack())
        s2_row = sb("s2_row", [P, NP])

        with ExitStack() as back:
            def bsb(name, shape, dt=F32):
                return back.enter_context(nc.sbuf_tensor(name, shape, dt))

            s_sb = bsb("s_sb", [P, 2, NT, W_ROW])
            sT = bsb("sT", [P, 2, 2, P])
            h2T = bsb("h2T", [D, NT, P])
            hhT = bsb("hhT", [D, NP])
            wT = bsb("wT", [D, D])
            a_col = bsb("a_col", [D, 1])
            a_rep = bsb("a_rep", [D, P])
            scored = bsb("scored", [P, NT, D])
            tails_set = sem("tails_set")
            col_loaded = sem("col_loaded")
            rep_ready = sem("rep_ready")
            wT_ready = sem("wT_ready")
            wT_used = sem("wT_used")
            h2T_ready = sem("h2T_ready")
            h2T_used = sem("h2T_used")
            hh_ready = sem("hh_ready")
            hh_used = sem("hh_used")
            hhT_ready = sem("hhT_ready")
            hhT_used = sem("hhT_used")
            s2_ready = sem("s2_ready")
            s2_used = sem("s2_used")

            with nc.Block() as block:
                @block.sync
                def _(sp):
                    full = (NT - 1) * P
                    sp.wait_ge(tails_set, 1)
                    for k, acc in enumerate((acc_src, acc_dst)):
                        sp.dma_start(s_sb[:, k, 0:NT - 1, :],
                                     acc[0:full, :].rearrange("(t p) w -> p t w", p=P)).then_inc(nodes_summed, 16)
                        sp.dma_start(s_sb[0:REST, k, NT - 1, :], acc[full:N, :]).then_inc(nodes_summed, 16)
                    sp.dma_start(a_col[:, :], a[0:1, D:2 * D].rearrange("o d -> d o"),
                                 allow_slow_non_contiguous=True).then_inc(col_loaded, 16)

                @block.vector
                def _(dve):
                    dve.memset(s_sb[:, :, NT - 1, :], 0.0).then_inc(tails_set, 1)
                    dve.wait_ge(nodes_summed, 64)
                    for t in range(NT):
                        dve.wait_ge(up_ready, t + 1)
                        chain(dve, dve.tensor_tensor(x1[:, t, :], psum[2 + t % 2][:, 0:D], x_sb[:, t, :], ALU.add))
                        dve.sem_inc(up_used, 1)
                        for k in range(2):
                            chain(dve, dve.scalar_tensor_tensor(
                                x1[:, t, :], b2_row[:, k * D:(k + 1) * D], s_sb[:, k, t, H:H + 1], x1[:, t, :],
                                ALU.mult, ALU.add))
                    layer_norm(dve, chain, x1, 1)
                    dve.wait_ge(col_loaded, 16)
                    dve.tensor_copy(a_rep[:, :], a_col[:, 0:1].to_broadcast([D, P])).then_inc(rep_ready, 1)
                    dve.wait_ge(wT_ready, 1)
                    dve.tensor_copy(wT[:, :], psum[4][0:D, 0:D]).then_inc(wT_used, 1)
                    for t in range(NT):
                        dve.wait_ge(h2T_ready, t + 1)
                        dve.tensor_copy(h2T[:, t, :], psum[t % 2][0:D, 0:P]).then_inc(h2T_used, 1)
                    for t in range(NT):
                        dve.wait_ge(hh_ready, t + 1)
                        dve.tensor_copy(hh[:, t, :], psum[2 + t % 2][:, 0:D]).then_inc(hh_used, 1)
                    dve.wait_ge(hh_used, NT)
                    chain(dve, dve.tensor_tensor(scored[:, :, :], hh[:, :, :],
                                                 a_row[:, 0:D].unsqueeze(1).to_broadcast([P, NT, D]), ALU.mult))
                    chain(dve, dve.tensor_reduce(from_src[:, :], scored[:, :, :], AX_X, ALU.add))

                @block.scalar
                def _(act):
                    for t in range(NT):
                        act.wait_ge(sT_ready, t + 1)
                        if t >= 2:
                            act.wait_ge(up_ready, t - 1)
                        nc.scalar.copy(sT[:, t % 2, :, :], psum[t % 2][:, 0:2 * P].rearrange("p (k n) -> p k n", k=2))\
                            .then_inc(sT_used, 1)
                    act.wait_ge(var_ready, 2)
                    nc.scalar.activation(std[:, :, :], mean_var[:, :, 1:2], ACT.Sqrt).then_inc(std_ready, 1)
                    for c, (lo, n) in enumerate(CH):
                        act.wait_ge(hhT_ready, c + 1)
                        nc.scalar.copy(hhT[:, lo:lo + n], psum[4 + c % 2][0:D, 0:n]).then_inc(hhT_used, 1)
                    for c, (lo, n) in enumerate(CH):
                        act.wait_ge(s2_ready, c + 1)
                        nc.scalar.copy(s2_row[:, lo:lo + n], psum[6 + c % 2][:, 0:n]).then_inc(s2_used, 1)

                @block.tensor
                def _(pe):
                    pe.wait_ge(nodes_summed, 64)
                    for t in range(NT + 1):
                        if t < NT:
                            if t >= 2:
                                pe.wait_ge(sT_used, t - 1)
                            for k in range(2):
                                last = pe.transpose(psum[t % 2][:, k * P:(k + 1) * P], s_sb[:, k, t, 0:H], ident[:, :])
                            last.then_inc(sT_ready, 1)
                        if t >= 1:
                            u = t - 1
                            pe.wait_ge(sT_used, u + 1)
                            if u >= 2:
                                pe.wait_ge(up_used, u - 1)
                            for k in range(2):
                                last = pe.matmul(psum[2 + u % 2][:, 0:D], sT[:, u % 2, k, :],
                                                 w2_sb[:, k * D:(k + 1) * D], start=(k == 0), stop=(k == 1))
                            last.then_inc(up_ready, 1)
                    pe.transpose(psum[4][0:D, 0:D], w_sb[:, :], ident[0:D, 0:D]).then_inc(wT_ready, 1)
                    pe.wait_ge(h_ready, 2)
                    for t in range(NT):
                        if t >= 2:
                            pe.wait_ge(h2T_used, t - 1)
                        pe.transpose(psum[t % 2][0:D, 0:P], h_sb[:, t, :], ident[:, :]).then_inc(h2T_ready, 1)
                    pe.wait_ge(wT_used, 1)
                    pe.wait_ge(h2T_used, NT)
                    for t in range(NT):
                        if t >= 2:
                            pe.wait_ge(hh_used, t - 1)
                        pe.matmul(psum[2 + t % 2][:, 0:D], h2T[:, t, :], wT[:, :], start=True, stop=True)\
                            .then_inc(hh_ready, 1)
                    for c, (lo, n) in enumerate(CH):
                        if c >= 2:
                            pe.wait_ge(hhT_used, c - 1)
                        pe.matmul(psum[4 + c % 2][0:D, 0:n], wT[:, :],
                                  h2T[:, :, :].rearrange("d t p -> d (t p)")[:, lo:lo + n], start=True, stop=True)\
                            .then_inc(hhT_ready, 1)
                    pe.wait_ge(rep_ready, 1)
                    for c, (lo, n) in enumerate(CH):
                        pe.wait_ge(hhT_used, c + 1)
                        if c >= 2:
                            pe.wait_ge(s2_used, c - 1)
                        pe.matmul(psum[6 + c % 2][:, 0:n], a_rep[:, :], hhT[:, lo:lo + n], start=True, stop=True)\
                            .then_inc(s2_ready, 1)

        cnt = sb("cnt", [P, 2, N])
        score = sb("score", [P, 2, N])
        best = sb("best", [P, 2, 4])
        total = sb("total", [P, 2, 2])
        gain = sb("gain", [P, 2, D])
        low = sb("low", [D, NP])
        act_out = sb("act_out", [D, NP])
        y = sb("y", [P, NT, D])
        cnt_loaded = [sem("cnt_loaded_0"), sem("cnt_loaded_1")]
        best_ready = sem("best_ready")
        weights_ready = sem("weights_ready")
        gain_ready = sem("gain_ready")
        spread = sem("spread")
        low_ready = sem("low_ready")
        exp_ready = sem("exp_ready")
        elu_ready = sem("elu_ready")
        yT_ready = sem("yT_ready")
        y_ready = sem("y_ready")
        scored_all = sem("scored_all")
        lrelu_ready = sem("lrelu_ready")
        written = sem("written")
        CN = [(lo, min(BANK, N - lo)) for lo in range(0, N, BANK)]
        assert len(CN) <= 7

        with nc.Block() as block:
            @block.sync
            def _(sp):
                for t in range(NT):
                    n = rows(t)
                    if t >= 2:
                        sp.wait_ge(gain_ready, t - 1)
                    sp.dma_start(cnt[0:n, t % 2, :],
                                 pairs[t * P * N:(t * P + n) * N, :].rearrange("(p d) o -> p (d o)", p=n))\
                        .then_inc(cnt_loaded[t % 2], 16)
                full = (NT - 1) * P
                sp.wait_ge(y_ready, NT)
                sp.dma_start(out[0:full, :].rearrange("(t p) d -> p t d", p=P), y[:, 0:NT - 1, :]).then_inc(written, 16)
                sp.dma_start(out[full:N, :], y[0:REST, NT - 1, :]).then_inc(written, 16)
                sp.wait_ge(written, 32)

            @block.vector
            def _(dve):
                def largest(t):
                    n, q = rows(t), t % 2
                    dve.wait_ge(cnt_loaded[q], 16 * (t // 2 + 1))
                    if t >= 2:
                        dve.wait_ge(spread, t - 1)
                    chain(dve, dve.tensor_scalar(score[0:n, q, :], cnt[0:n, q, :], 0.0, -FAR, ALU.is_equal, ALU.mult))
                    chain(dve, dve.tensor_tensor_reduce(score[0:n, q, :], score[0:n, q, :], s2_row[0:n, 0:N], 1.0,
                                                        -3.0 * FAR, ALU.add, ALU.max, best[0:n, q, 0:1]))
                    chain(dve, dve.tensor_tensor(best[0:n, q, 1:2], best[0:n, q, 0:1], from_src[0:n, t:t + 1], ALU.add))
                    chain(dve, dve.tensor_scalar(best[0:n, q, 2:3], best[0:n, q, 1:2], -SLOPE, None, ALU.mult))
                    dve.scalar_tensor_tensor(best[0:n, q, 3:4], best[0:n, q, 1:2], -1.0, best[0:n, q, 2:3],
                                             ALU.mult, ALU.min).then_inc(best_ready, 1)

                def leaky(t):
                    n, q = rows(t), t % 2
                    dve.wait_ge(scored_all, t + 1)
                    dve.scalar_tensor_tensor(score[0:n, q, :], score[0:n, q, :], SLOPE, score[0:n, q, :],
                                             ALU.mult, ALU.max).then_inc(lrelu_ready, 1)

                def weigh(t):
                    n, q = rows(t), t % 2
                    dve.wait_ge(weights_ready, t + 1)
                    chain(dve, dve.tensor_tensor_reduce(score[0:n, q, :], score[0:n, q, :], cnt[0:n, q, :], 1.0,
                                                        0.0, ALU.mult, ALU.add, total[0:n, q, 0:1]))
                    chain(dve, dve.tensor_scalar(total[0:n, q, 0:1], total[0:n, q, 0:1], 0.5, None, ALU.max))
                    chain(dve, dve.reciprocal(total[0:n, q, 1:2], total[0:n, q, 0:1]))
                    dve.tensor_scalar(gain[0:n, q, :], hh[0:n, t, :], total[0:n, q, 1:2], None,
                                      ALU.mult).then_inc(gain_ready, 1)

                largest(0)
                leaky(0)
                for t in range(NT):
                    if t + 1 < NT:
                        largest(t + 1)
                    weigh(t)
                    if t + 1 < NT:
                        leaky(t + 1)
                dve.wait_ge(spread, NT)
                dve.memset(act_out[:, N:NP], 0.0)
                for c, (lo, n) in enumerate(CN):
                    dve.tensor_scalar(low[:, lo:lo + n], psum[c][0:D, 0:n], 0.0, None, ALU.min).then_inc(low_ready, 1)
                for c, (lo, n) in enumerate(CN):
                    dve.wait_ge(exp_ready, c + 1)
                    chain(dve, dve.tensor_scalar(low[:, lo:lo + n], low[:, lo:lo + n], -1.0, None, ALU.add))
                    dve.scalar_tensor_tensor(act_out[:, lo:lo + n], psum[c][0:D, 0:n], 0.0, low[:, lo:lo + n],
                                             ALU.max, ALU.add).then_inc(elu_ready, 1)
                for t in range(NT):
                    dve.wait_ge(yT_ready, t + 1)
                    dve.tensor_tensor(y[:, t, :], psum[t % 2][:, 0:D], x1[:, t, :], ALU.add).then_inc(y_ready, 1)

            @block.scalar
            def _(act):
                for t in range(NT):
                    n, q = rows(t), t % 2
                    act.wait_ge(best_ready, t + 1)
                    nc.scalar.activation(score[0:n, q, :], score[0:n, q, :], ACT.Identity,
                                         bias=from_src[0:n, t:t + 1]).then_inc(scored_all, 1)
                    act.wait_ge(lrelu_ready, t + 1)
                    nc.scalar.activation(score[0:n, q, :], score[0:n, q, :], ACT.Exp, bias=best[0:n, q, 3:4])\
                        .then_inc(weights_ready, 1)
                for c, (lo, n) in enumerate(CN):
                    act.wait_ge(low_ready, c + 1)
                    nc.scalar.activation(low[:, lo:lo + n], low[:, lo:lo + n], ACT.Exp).then_inc(exp_ready, 1)

            @block.tensor
            def _(pe):
                for t in range(NT):
                    n, q = rows(t), t % 2
                    pe.wait_ge(gain_ready, t + 1)
                    for c, (lo, m) in enumerate(CN):
                        last = pe.matmul(psum[c][0:D, 0:m], gain[0:n, q, :], score[0:n, q, lo:lo + m],
                                         start=(t == 0), stop=(t == NT - 1))
                    last.then_inc(spread, 1)
                pe.wait_ge(elu_ready, len(CN))
                for t in range(NT):
                    if t >= 2:
                        pe.wait_ge(y_ready, t - 1)
                    pe.transpose(psum[t % 2][:, 0:D], act_out[:, t * P:(t + 1) * P], ident[0:D, 0:D])\
                        .then_inc(yT_ready, 1)


INPUTS = ["x", "src", "dst", "edge_weight", "L0_gnn_W1", "L0_gnn_b1", "L0_gnn_Wt", "L0_gnn_bt", "L0_gnn_W2",
          "L0_gnn_b2", "L1_gnn_W", "L1_gnn_a"]


def constants(N, E):
    rows = max(k for k in range(1, P + 1) if E % k == 0)
    p = np.arange(rows)
    return {
        "identity": np.eye(P, dtype=np.float32),
        "below": np.tril(np.ones((rows, rows), np.float32), -1),
        "spare": np.stack([N + p, N + p, N * N + p], 1).astype(np.float32),
    }


def kernel(**inputs):
    import concourse.bacc as bacc
    from concourse.bass_utils import run_bass_kernel_spmd

    arrays = {name: np.ascontiguousarray(inputs[name]) for name in INPUTS}
    N, D = arrays["x"].shape
    arrays |= constants(N, arrays["src"].shape[0])
    nc = bacc.Bacc("TRN2", target_bir_lowering=False, num_devices=1)
    feeds, args = {}, []
    for name, value in arrays.items():
        feeds[f"in_{name}"] = value
        args.append(nc.dram_tensor(f"in_{name}", value.shape, mybir.dt.from_np(value.dtype), kind="ExternalInput").ap())
    args.append(nc.dram_tensor("out_x", (N, D), F32, kind="ExternalOutput").ap())
    build(nc, *args)
    got = run_bass_kernel_spmd(nc, [feeds], core_ids=[0])
    return got.results[0]["out_x"]
```

```python
from contextlib import ExitStack

import numpy as np

import concourse.bass as bass
from concourse import mybir

P = 128
F32 = mybir.dt.float32
I32 = mybir.dt.int32
U8 = mybir.dt.uint8
BF16 = mybir.dt.bfloat16
F16 = mybir.dt.float16
ALU = mybir.AluOpType
ACT = mybir.ActivationFunctionType
AX_X = mybir.AxisListType.X
EPS = 1e-5
SLOPE = 0.2
FAR = 1e30
BANK = 512
WIN = 48
U = 4
Q4 = 4
MAX_COUNT = 255.0


def build(nc, x, src, dst, edge_weight, W1, b1, Wt, bt, W2, b2, W, a, identity, below, spare, steps, out):
    N, D = x.shape
    E = src.shape[0]
    H = W1.shape[1]
    NT = (N + P - 1) // P
    REST = N - (NT - 1) * P
    EP = max(k for k in range(1, P + 1) if E % k == 0)
    ET = E // EP
    G = ET // U
    GE = U * EP
    R = G // Q4
    NB = NT * WIN
    NC = -(-(N + WIN) // 4) * 4
    ROWS_IN = 100
    CI = ET // ROWS_IN
    W_ROW = H + 1
    assert ET == U * G and G == Q4 * R and G % ROWS_IN == 0 and ET % ROWS_IN == 0
    assert U * H == BANK and GE <= BANK and R >= 3 and 2 * D == H

    acc_src = [nc.dram_tensor(f"acc_src_{u}", (N + EP, W_ROW), F32, kind="Internal").ap() for u in range(U)]
    acc_dst = nc.dram_tensor("acc_dst", (N + EP, W_ROW), F32, kind="Internal").ap()
    pairs = nc.dram_tensor("pairs", (N * N + EP, 1), F32, kind="Internal").ap()
    table_p = nc.dram_tensor("table_p", (N, H), F32, kind="Internal").ap()
    first_node = nc.dram_tensor("first_node", (G,), I32, kind="Internal").ap()
    node_span = nc.dram_tensor("node_span", (G,), F32, kind="Internal").ap()
    table_q = nc.dram_tensor("table_q", (NC, H), F32, kind="Internal").ap()

    def rows(t):
        return P if t < NT - 1 else REST

    with ExitStack() as ctx:
        def sb(name, shape, dt=F32):
            return ctx.enter_context(nc.sbuf_tensor(name, shape, dt))

        def sem(name):
            return ctx.enter_context(nc.semaphore(name))

        ident = sb("ident", [P, P])
        x_sb = sb("x_sb", [P, NT, D])
        w2_sb = sb("w2_sb", [H, 2 * D])
        b2_row = sb("b2_row", [P, 2 * D])
        w_sb = sb("w_sb", [D, D])
        a_row = sb("a_row", [P, 2 * D])
        stats = sb("stats", [P, NT, 6])
        mean_var = sb("mean_var", [P, NT, 2])
        std = sb("std", [P, NT, 1])
        rstd = sb("rstd", [P, NT, 1])
        until_nodes = ctx.enter_context(ExitStack())
        accT = until_nodes.enter_context(nc.sbuf_tensor("accT", [H, NC], F32, side="right"))
        cnt_row = until_nodes.enter_context(nc.sbuf_tensor("cnt_row", [1, NC], F32, side="right"))
        until_summed = ctx.enter_context(ExitStack())
        edges = until_summed.enter_context(nc.sbuf_tensor("edges", [EP, 6, ET], F32, side="right"))
        firsts_i = sb("firsts_i", [1, G], I32)
        flag = sb("flag", [1, 4])
        flag_i = sb("flag_i", [1, 1], I32)
        cols = sb("cols", [P, NT, NC], U8)
        psum = [ctx.enter_context(nc.psum_tensor(f"ps{i}", [P, BANK], F32)) for i in range(8)]

        loaded = sem("loaded")
        dve_step = sem("dve_step")
        zeros_set = sem("zeros_set")
        tail_set = sem("tail_set")
        zeroed = sem("zeroed")
        std_ready = sem("std_ready")
        var_ready = sem("var_ready")
        h_ready = sem("h_ready")
        hT_ready = sem("hT_ready")
        hT_used = sem("hT_used")
        pq_ready = sem("pq_ready")
        pq_copied = sem("pq_copied")
        stored = [sem("stored_0"), sem("stored_1")]

        class Chain:

            def __init__(self):
                self.n = 0

            def __call__(self, eng, ins):
                self.n += 1
                ins.then_inc(dve_step, 1)
                eng.wait_ge(dve_step, self.n)

        chain = Chain()

        def layer_norm(dve, step, rows_in, h_sb, which):
            for t in range(NT):
                last = dve.bn_stats(stats[:, t, :], rows_in[:, t, :])
            step(dve, last)
            for t in range(NT):
                last = dve.bn_aggr(mean_var[:, t, :], stats[:, t, :])
            step(dve, last)
            dve.tensor_scalar(mean_var[:, :, 1:2], mean_var[:, :, 1:2], EPS, None,
                              ALU.add).then_inc(var_ready, 1)
            dve.wait_ge(std_ready, 1 + which)
            step(dve, dve.reciprocal(rstd[:, :, :], std[:, :, :]))
            step(dve, dve.tensor_tensor(h_sb[:, :, :], rows_in[:, :, :],
                                        mean_var[:, :, 0:1].to_broadcast([P, NT, D]), ALU.subtract))
            step(dve, dve.tensor_tensor(h_sb[:, :, :], h_sb[:, :, :],
                                        rstd[:, :, :].to_broadcast([P, NT, D]), ALU.mult))
            dve.tensor_scalar(h_sb[:, :, :], h_sb[:, :, :], 0.0, None, ALU.max).then_inc(h_ready, 1)

        with ExitStack() as early:
            def esb(name, shape, dt=F32):
                return early.enter_context(nc.sbuf_tensor(name, shape, dt))

            zeros = esb("zeros", [P, N])
            h_sb = esb("h_sb", [P, NT, D])
            w1a = esb("w1a", [D + 1, H])
            w1b = esb("w1b", [D, H])
            hT = esb("hT", [D + 1, NT, P])
            pq = esb("pq", [P, 2, 2, H])
            raw_i = esb("raw_i", [ROWS_IN, 2, CI * EP], I32)
            raw = esb("raw", [ROWS_IN, 3, CI * EP])
            by_group = esb("by_group", [ROWS_IN, G // ROWS_IN * GE], I32)
            ends = esb("ends", [ROWS_IN, 4, G // ROWS_IN])
            first_i = esb("first_i", [ROWS_IN, G // ROWS_IN], I32)
            firsts_all = esb("firsts_all", [EP, G], I32)
            firsts_f = esb("firsts_f", [EP, G])
            spans = esb("spans", [1, G])
            bits = esb("bits", [EP, ET], I32)
            raw_loaded = sem("raw_loaded")
            raw_ready = sem("raw_ready")
            ends_ready = sem("ends_ready")
            ends_stored = sem("ends_stored")
            firsts_loaded = sem("firsts_loaded")
            turned = sem("turned")
            turned_used = sem("turned_used")

            with nc.Block() as block:
                def windows(dve):
                    dve.wait_ge(raw_loaded, 64)
                    groups = by_group[:, :].rearrange("p (g e) -> p g e", e=GE)
                    dve.tensor_reduce(ends[:, 0, :], groups, AX_X, ALU.max)
                    chain(dve, dve.tensor_reduce(ends[:, 1, :], groups, AX_X, ALU.min))
                    dve.tensor_tensor(ends[:, 2, :], ends[:, 0, :], ends[:, 1, :], ALU.subtract)
                    dve.tensor_copy(first_i[:, :], ends[:, 1, :]).then_inc(ends_ready, 1)
                    dve.tensor_copy(raw[:, 0:2, :], raw_i[:, :, :]).then_inc(raw_ready, 1)

                def place_edges(dve):
                    n = 0
                    for k, to in enumerate((0, 5, 4)):
                        for c in range(0, CI, U):
                            n += 1
                            dve.wait_ge(turned, n)
                            ins = dve.tensor_copy(edges[:, to, c * ROWS_IN:(c + U) * ROWS_IN],
                                                  psum[4 + n % 4][0:EP, 0:U * ROWS_IN])
                            ins.then_inc(turned_used, 1)
                    dve.wait_ge(turned_used, n)
                    dve.wait_ge(firsts_loaded, 48)
                    dve.tensor_copy(bits[:, :], edges[:, 0, :])
                    dve.tensor_reduce(flag[:, 0:1], spans[:, :], AX_X, ALU.max)
                    chain(dve, dve.tensor_copy(firsts_f[:, :], firsts_all[:, :]))
                    dve.tensor_tensor(edges[:, 3, :].rearrange("p (g u) -> p g u", u=U),
                                      edges[:, 5, :].rearrange("p (g u) -> p g u", u=U),
                                      firsts_f[:, :].unsqueeze(2).to_broadcast([EP, G, U]), ALU.subtract)
                    chain(dve, dve.tensor_scalar(bits[:, :], bits[:, :], P - 1, None, ALU.bitwise_and))
                    chain(dve, dve.tensor_copy(edges[:, 1, :], bits[:, :]))
                    chain(dve, dve.tensor_tensor(edges[:, 2, :], edges[:, 0, :], edges[:, 1, :], ALU.subtract))
                    chain(dve, dve.scalar_tensor_tensor(edges[:, 2, :], edges[:, 2, :], WIN / P, edges[:, 3, :],
                                                        ALU.mult, ALU.add))

                def copy_pq(dve, t):
                    dve.wait_ge(pq_ready, t + 1)
                    if t >= 2:
                        dve.wait_ge(stored[t % 2], 32 * (t // 2))
                    dve.tensor_copy(pq[:, t % 2, :, :].rearrange("p a h -> p (a h)"),
                                    psum[2 + t % 2][:, 0:2 * H]).then_inc(pq_copied, 1)

                @block.sync
                def _(sp):
                    full = (NT - 1) * P
                    sp.wait_ge(tail_set, 1)
                    loads = [
                        (x_sb[:, 0:NT - 1, :], x[0:full, :].rearrange("(t p) d -> p t d", p=P)),
                        (x_sb[0:REST, NT - 1, :], x[full:N, :]),
                        (ident[:, :], identity),
                        (w1a[0:D, :], W1[0:D, :]),
                        (w1a[D:D + 1, :], b1.rearrange("(o n) -> o n", o=1)),
                        (w1b[:, :], W1[D:2 * D, :]),
                        (w2_sb[:, :], W2),
                        (b2_row[:, :], b2.rearrange("(o n) -> o n", o=1).to_broadcast([P, 2 * D])),
                        (w_sb[:, :], W),
                        (a_row[:, :], a.to_broadcast([P, 2 * D])),
                    ]
                    for to, of in (
                        (by_group[:, :], dst.rearrange("(p e) -> p e", p=ROWS_IN)),
                        (raw_i[:, 0, :].rearrange("p (c e) -> p c e", c=CI),
                         src.rearrange("(c p e) -> p c e", c=CI, p=ROWS_IN)),
                        (raw_i[:, 1, :].rearrange("p (c e) -> p c e", c=CI),
                         dst.rearrange("(c p e) -> p c e", c=CI, p=ROWS_IN)),
                        (raw[:, 2, :].rearrange("p (c e) -> p c e", c=CI),
                         edge_weight.rearrange("(c p e) -> p c e", c=CI, p=ROWS_IN)),
                    ):
                        sp.dma_start(to, of).then_inc(raw_loaded, 16)
                    for to, of in loads:
                        sp.dma_start(to, of).then_inc(loaded, 16)
                    sp.wait_ge(ends_ready, 1)
                    sp.dma_start(first_node.rearrange("(p g) -> p g", p=ROWS_IN), first_i[:, :])\
                        .then_inc(ends_stored, 16)
                    sp.dma_start(node_span.rearrange("(p g) -> p g", p=ROWS_IN), ends[:, 2, :])\
                        .then_inc(ends_stored, 16)
                    sp.wait_ge(ends_stored, 32)
                    for to, of in (
                        (firsts_i[:, :], first_node.rearrange("(o g) -> o g", o=1)),
                        (firsts_all[:, :], first_node.rearrange("(o g) -> o g", o=1).to_broadcast([EP, G])),
                        (spans[:, :], node_span.rearrange("(o g) -> o g", o=1)),
                    ):
                        sp.dma_start(to, of).then_inc(firsts_loaded, 16)
                    assert len(loads) == 10
                    for t in range(NT):
                        n = rows(t)
                        sp.wait_ge(pq_copied, t + 1)
                        sp.dma_start(table_p[t * P:t * P + n, :], pq[0:n, t % 2, 0, :]).then_inc(stored[t % 2], 16)
                        sp.dma_start(table_q[t * P:t * P + n, :], pq[0:n, t % 2, 1, :]).then_inc(stored[t % 2], 16)
                    sp.wait_ge(stored[0], 32 * ((NT + 1) // 2))
                    sp.wait_ge(stored[1], 32 * (NT // 2))

                @block.gpsimd
                def _(pool):
                    pool.memset(zeros[:, :], 0.0).then_inc(zeros_set, 1)
                    pool.memset(accT[:, :], 0.0)
                    pool.memset(cnt_row[:, :], 0.0)
                    pool.memset(cols[:, :, :].rearrange("p t n -> p (t n)").bitcast(I32), 0)

                @block.scalar
                def _(act):
                    act.wait_ge(zeros_set, 1)
                    n = 0
                    for acc in acc_src:
                        for k in range((N + EP) // EP):
                            act.dma_start(acc[k * EP:(k + 1) * EP, :], zeros[0:EP, 0:W_ROW]).then_inc(zeroed, 16)
                            n += 1
                    act.dma_start(table_q[N:NC, :], zeros[0:NC - N, 0:H]).then_inc(zeroed, 16)
                    n += 1
                    act.wait_ge(var_ready, 1)
                    nc.scalar.activation(std[:, :, :], mean_var[:, :, 1:2], ACT.Sqrt).then_inc(std_ready, 1)
                    act.wait_ge(zeroed, 16 * n)

                @block.vector
                def _(dve):
                    dve.memset(x_sb[:, NT - 1, :], 0.0).then_inc(tail_set, 1)
                    dve.memset(hT[D:D + 1, :, :], 1.0)
                    windows(dve)
                    dve.wait_ge(loaded, 160)
                    layer_norm(dve, chain, x_sb, h_sb, 0)
                    for t in range(NT):
                        dve.wait_ge(hT_ready, t + 1)
                        dve.tensor_copy(hT[0:D, t, :], psum[t % 2][0:D, 0:P]).then_inc(hT_used, 1)
                        if t >= 1:
                            copy_pq(dve, t - 1)
                    copy_pq(dve, NT - 1)
                    place_edges(dve)

                @block.tensor
                def _(pe):
                    pe.wait_ge(loaded, 160)
                    pe.wait_ge(h_ready, 1)
                    for t in range(NT + 1):
                        if t < NT:
                            if t >= 2:
                                pe.wait_ge(hT_used, t - 1)
                            pe.transpose(psum[t % 2][0:D, 0:P], h_sb[:, t, :], ident[:, :]).then_inc(hT_ready, 1)
                        if t >= 1:
                            u = t - 1
                            pe.wait_ge(hT_used, u + 1)
                            if u >= 2:
                                pe.wait_ge(pq_copied, u - 1)
                            pe.matmul(psum[2 + u % 2][:, 0:H], hT[:, u, :], w1a[:, :], start=True, stop=True)
                            pe.matmul(psum[2 + u % 2][:, H:2 * H], hT[0:D, u, :], w1b[:, :],
                                      start=True, stop=True).then_inc(pq_ready, 1)
                    pe.wait_ge(raw_ready, 1)
                    n = 0
                    for k in range(3):
                        for c in range(0, CI, U):
                            n += 1
                            if n > 4:
                                pe.wait_ge(turned_used, n - 4)
                            for v in range(U):
                                last = pe.transpose(psum[4 + n % 4][0:EP, v * ROWS_IN:(v + 1) * ROWS_IN],
                                                    raw[:, k, (c + v) * EP:(c + v + 1) * EP],
                                                    ident[0:ROWS_IN, 0:ROWS_IN])
                            last.then_inc(turned, 1)

        def rounds(eng, work, n):
            work(0)
            with eng.Fori(1, n - 1) as r:
                work(r)
            work(n - 1)

        def known(r, n):
            return isinstance(r, int) and r == n

        def past(eng, what, n):
            if not isinstance(n, int) or n > 0:
                eng.wait_ge(what, n)

        with ExitStack() as mid:
            def msb(name, shape, dt=F32):
                return mid.enter_context(nc.sbuf_tensor(name, shape, dt))

            def msem(name):
                return mid.enter_context(nc.semaphore(name))

            wtbt = msb("wtbt", [2, H])
            steps_sb = msb("steps_sb", [EP, NB], F16)
            win_f = msb("win_f", [EP, WIN])
            ones = msb("ones", [EP, 1])
            lower = msb("lower", [EP, EP])
            spare_sb = msb("spare_sb", [EP, 3])
            key = msb("key", [EP, Q4, 5, U])
            key_i = msb("key_i", [EP, Q4, U], I32)
            rows_p = msb("rows_p", [EP, Q4, U, H])
            t_rows = msb("t_rows", [2, Q4, GE])
            window_q = msb("window_q", [WIN, Q4, H])
            to_row = msb("to_row", [EP, Q4, U], I32)
            sums = msb("sums", [EP, Q4, U, W_ROW])
            src_hot = msb("src_hot", [EP, 2, U, P], BF16)
            pair_hot = msb("pair_hot", [EP, 2, U, NB], BF16)
            dst_hot = msb("dst_hot", [EP, 2, U, WIN])
            dst_hotT = msb("dst_hotT", [WIN, 2, GE])
            equal = msb("equal", [EP, 2, U, EP])
            earlier = msb("earlier", [EP, 2, U, EP])
            n_earlier = msb("n_earlier", [EP, 2, U])
            move = msb("move", [EP, 2, U])
            temb = msb("temb", [EP, 2, U, H])
            hid = msb("hid", [EP, 2, U, H])

            ps_pair = psum[0:2]
            ps_src, ps_temb, ps_hotT, ps_pre, ps_sum, ps_dst = psum[2:8]
            AT_CNT, AT_MULT = 64, 128
            CHUNKS = [(b, min(BANK // WIN, NT - b)) for b in range(0, NT, BANK // WIN)]
            NCH = len(CHUNKS)
            assert NCH == 3

            constants_loaded = msem("constants_loaded")
            ones_set = msem("ones_set")
            t_loaded = [msem(f"t_loaded_{q}") for q in range(Q4)]
            q_loaded = [msem(f"q_loaded_{q}") for q in range(Q4)]
            fetched = [msem(f"fetched_{q}") for q in range(Q4)]
            added = [msem(f"added_{u}") for u in range(U)]
            keys_ready = msem("keys_ready")
            dst_hot_ready = msem("dst_hot_ready")
            pair_hot_ready = msem("pair_hot_ready")
            turned_src = msem("turned_src")
            equal_ready = msem("equal_ready")
            rows_ready = msem("rows_ready")
            temb_in = msem("temb_in")
            temb_ready = msem("temb_ready")
            hotT_in = msem("hotT_in")
            hotT_ready = msem("hotT_ready")
            q_ready = msem("q_ready")
            pre_ready = msem("pre_ready")
            hid_ready = msem("hid_ready")
            pairs_ready = msem("pairs_ready")
            pairs_used = msem("pairs_used")
            summed = msem("summed")
            sums_ready = msem("sums_ready")
            dst_used = msem("dst_used")
            own = msem("own")
            pool_passed = msem("pool_passed")
            pe_passed = msem("pe_passed")
            OWN = 2

            def after(r, q):
                return (r + q // Q4, q % Q4)

            def exists(r, q):
                return not (isinstance(r, int) and r * Q4 + q >= G)

            with nc.Block() as block:
                @block.sync
                def _(sp):
                    for to, of in (
                        (wtbt[0:1, :], Wt),
                        (wtbt[1:2, :], bt.rearrange("(o n) -> o n", o=1)),
                        (steps_sb[:, :], steps),
                        (lower[:, :], below),
                        (spare_sb[:, :], spare),
                    ):
                        sp.dma_start(to, of).then_inc(constants_loaded, 16)
                    sp.wait_ge(ones_set, 1)
                    weights = edge_weight.rearrange("(o e) -> o e", o=1)

                    def work(r):
                        _, firsts = nc.values_load_multi_w_load_instructions(
                            firsts_i[0:1, bass.ds(r * Q4, Q4)], engines=[mybir.EngineType.SP],
                            min_val=0, max_val=N - 1)
                        for q in range(Q4):
                            g = r * Q4 + q
                            past(sp, temb_in, g - Q4 + 1)
                            sp.dma_start(t_rows[0:1, q, :], weights[:, bass.ds(g * GE, GE)]).then_inc(t_loaded[q], 16)
                            past(sp, q_ready, g - Q4 + 1)
                            sp.dma_start(window_q[:, q, :], table_q[bass.ds(firsts[q], WIN), :])\
                                .then_inc(q_loaded[q], 16)

                    rounds(sp, work, R)

                @block.gpsimd
                def _(pool):
                    def apart():
                        pool.sem_inc(pool_passed, 1)

                    def fetch(r, q):
                        g = r * Q4 + q
                        pool.wait_ge(keys_ready, g + 1)
                        past(pool, hid_ready, g - Q4 + 1)
                        apart()
                        for u in range(U):
                            pool.indirect_dma_start(
                                rows_p[:, q, u, :], None, table_p,
                                bass.IndirectOffsetOnAxis(ap=key_i[:, q, u:u + 1], axis=0)).then_inc(fetched[q], 16)

                    def add(r, q):
                        g = r * Q4 + q
                        pool.wait_ge(rows_ready, g + 1)
                        pool.wait_ge(sums_ready, g + 1)
                        pool.wait_ge(dst_used, g + 1)
                        apart()
                        for u in range(U):
                            past(pool, added[u], g * 16)
                            apart()
                            pool.indirect_dma_start(
                                acc_src[u], bass.IndirectOffsetOnAxis(ap=to_row[:, q, u:u + 1], axis=0),
                                sums[:, q, u, :], None, compute_op=ALU.add).then_inc(added[u], 16)

                    fetch(0, 0)
                    fetch(0, 1)

                    def work(r):
                        for q in range(Q4):
                            if exists(r, q + 2):
                                fetch(*after(r, q + 2))
                            add(r, q)

                    rounds(pool, work, R)
                    for u in range(U):
                        pool.wait_ge(added[u], 16 * G)

                @block.vector
                def _(dve):
                    dve.memset(t_rows[:, :, :], 1.0).then_inc(ones_set, 1)
                    dve.memset(ones[:, :], 1.0)
                    dve.wait_ge(constants_loaded, 5 * 16)
                    dve.tensor_copy(win_f[:, :], steps_sb[:, 0:WIN]).then_inc(ones_set, 1)
                    dve.wait_ge(ones_set, 2)

                    def step(ins, r, q, k):
                        ins.then_inc(own, 1)
                        dve.wait_ge(own, (r * Q4 + q) * OWN + k)

                    def take_keys(r, q):
                        cols_of = bass.ds(r * (Q4 * U) + q * U, U)
                        if not known(r, 0):
                            dve.wait_ge(fetched[q], r * (U * 16))
                        dve.tensor_copy(key_i[:, q, :], edges[:, 0, cols_of])
                        dve.tensor_copy(key[:, q, :, :], edges[:, 0:5, cols_of]).then_inc(keys_ready, 1)

                    def one_hots(r, q):
                        g, s = r * Q4 + q, q % 2
                        dve.wait_ge(keys_ready, g + 1)
                        past(dve, summed, g - 1)
                        dve.tensor_tensor(dst_hot[:, s, :, :], win_f[:, :].unsqueeze(1).to_broadcast([EP, U, WIN]),
                                          key[:, q, 3, :].unsqueeze(2).to_broadcast([EP, U, WIN]), ALU.is_equal)\
                            .then_inc(dst_hot_ready, 1)
                        for u in range(U):
                            dve.tensor_scalar(src_hot[:, s, u, :], steps_sb[:, 0:P], key[:, q, 1, u:u + 1], None,
                                              ALU.is_equal)
                            last = dve.tensor_scalar(pair_hot[:, s, u, :], steps_sb[:, :], key[:, q, 2, u:u + 1],
                                                     None, ALU.is_equal)
                        last.then_inc(pair_hot_ready, 1)

                    def equals(r, q):
                        g, s = r * Q4 + q, q % 2
                        dve.wait_ge(turned_src, g + 1)
                        dve.tensor_tensor(equal[:, s, :, :], ps_src[0:EP, 0:GE].rearrange("p (u e) -> p u e", u=U),
                                          key[:, q, 0, :].unsqueeze(2).to_broadcast([EP, U, EP]), ALU.is_equal)
                        for u in range(U):
                            last = dve.scalar_tensor_tensor(
                                earlier[:, s, u, :], ps_src[0:EP, u * EP:(u + 1) * EP], key[:, q, 0, u:u + 1],
                                lower[:, :], ALU.is_equal, ALU.mult, accum_out=n_earlier[:, s, u:u + 1])
                        last.then_inc(equal_ready, 1)
                        step(dve.tensor_tensor(move[:, s, :], spare_sb[:, 0:1].to_broadcast([EP, U]),
                                               key[:, q, 0, :], ALU.subtract), r, q, 1)
                        step(dve.scalar_tensor_tensor(move[:, s, :], n_earlier[:, s, :], 0.5, move[:, s, :],
                                                      ALU.is_gt, ALU.mult), r, q, 2)
                        if not known(r, 0):
                            for u in range(U):
                                dve.wait_ge(added[u], (g - Q4 + 1) * 16)
                        dve.tensor_tensor(to_row[:, q, :], move[:, s, :], key[:, q, 0, :],
                                          ALU.add).then_inc(rows_ready, 1)

                    def before_silu(r, q):
                        g = r * Q4 + q
                        dve.wait_ge(fetched[q], (r + 1) * (U * 16))
                        dve.wait_ge(q_ready, g + 1)
                        dve.tensor_tensor(rows_p[:, q, :, :], rows_p[:, q, :, :],
                                          ps_pre[0:EP, :].rearrange("p (u h) -> p u h", u=U),
                                          ALU.add).then_inc(pre_ready, 1)

                    def add_pairs(r, q, first):
                        g = r * Q4 + q
                        past(dve, pairs_used, g * NCH)
                        for c, (b, n) in enumerate(CHUNKS):
                            dve.wait_ge(pairs_ready, g * NCH + (c + 1))
                            onto = cols[:, b:b + n, bass.ds(first, WIN)]
                            dve.tensor_tensor(onto, onto, ps_pair[(NCH * q + c) % 2][:, 0:n * WIN]
                                              .rearrange("p (b w) -> p b w", b=n), ALU.add).then_inc(pairs_used, 1)

                    def add_dst(r, q, first):
                        g = r * Q4 + q
                        dve.wait_ge(summed, g + 1)
                        past(dve, dst_used, g)
                        dve.tensor_copy(sums[:, q, :, H], ps_dst[0:EP, AT_MULT:AT_MULT + U])
                        onto = accT[:, bass.ds(first, WIN)]
                        dve.tensor_tensor(onto, onto, ps_dst[:, 0:WIN], ALU.add)
                        onto = cnt_row[:, bass.ds(first, WIN)]
                        dve.tensor_tensor(onto, onto, ps_dst[0:1, AT_CNT:AT_CNT + WIN], ALU.add)\
                            .then_inc(dst_used, 1)

                    take_keys(0, 0)
                    take_keys(0, 1)
                    one_hots(0, 0)
                    equals(0, 0)

                    def work(r):
                        _, firsts = nc.values_load_multi_w_load_instructions(
                            firsts_i[0:1, bass.ds(r * Q4, Q4)], engines=[mybir.EngineType.DVE],
                            min_val=0, max_val=N - 1)
                        for q in range(Q4):
                            if exists(r, q + 2):
                                take_keys(*after(r, q + 2))
                            before_silu(r, q)
                            if exists(r, q + 1):
                                one_hots(*after(r, q + 1))
                            add_pairs(r, q, firsts[q])
                            if exists(r, q + 1):
                                equals(*after(r, q + 1))
                            add_dst(r, q, firsts[q])

                    rounds(dve, work, R)

                @block.scalar
                def _(act):
                    def time_part(r, q):
                        g, s = r * Q4 + q, q % 2
                        act.wait_ge(temb_in, g + 1)
                        past(act, q_ready, g - 1)
                        nc.scalar.activation(temb[:, s, :, :], ps_temb[0:EP, :].rearrange("p (u h) -> p u h", u=U),
                                             ACT.Silu).then_inc(temb_ready, 1)
                        act.wait_ge(hotT_in, g + 1)
                        nc.scalar.copy(dst_hotT[:, s, :], ps_hotT[0:WIN, 0:GE]).then_inc(hotT_ready, 1)

                    def hidden(r, q):
                        g, s = r * Q4 + q, q % 2
                        act.wait_ge(pre_ready, g + 1)
                        past(act, summed, g - 1)
                        nc.scalar.activation(hid[:, s, :, :], rows_p[:, q, :, :], ACT.Silu).then_inc(hid_ready, 1)

                    def take_sums(r, q):
                        g = r * Q4 + q
                        act.wait_ge(summed, g + 1)
                        if not known(r, 0):
                            for u in range(U):
                                act.wait_ge(added[u], (g - Q4 + 1) * 16)
                        nc.scalar.copy(sums[:, q, :, 0:H], ps_sum[0:EP, :].rearrange("p (u h) -> p u h", u=U))\
                            .then_inc(sums_ready, 1)

                    time_part(0, 0)

                    def work(r):
                        for q in range(Q4):
                            hidden(r, q)
                            if exists(r, q + 1):
                                time_part(*after(r, q + 1))
                            take_sums(r, q)

                    rounds(act, work, R)

                @block.tensor
                def _(pe):
                    pe.wait_ge(constants_loaded, 5 * 16)
                    pe.wait_ge(ones_set, 2)

                    def turn(r, q):
                        g, s = r * Q4 + q, q % 2
                        pe.wait_ge(t_loaded[q], (r + 1) * 16)
                        past(pe, temb_ready, g)
                        for u in range(U):
                            last = pe.matmul(ps_temb[0:EP, u * H:(u + 1) * H], t_rows[:, q, u * EP:(u + 1) * EP],
                                             wtbt[:, :], start=True, stop=True)
                        last.then_inc(temb_in, 1)
                        pe.wait_ge(dst_hot_ready, g + 1)
                        past(pe, hotT_ready, g)
                        pe.sem_inc(pe_passed, 1)
                        for u in range(U):
                            last = pe.transpose(ps_hotT[0:WIN, u * EP:(u + 1) * EP], dst_hot[:, s, u, :],
                                                ident[0:EP, 0:EP])
                        last.then_inc(hotT_in, 1)
                        pe.wait_ge(keys_ready, g + 1)
                        past(pe, equal_ready, g)
                        for u in range(U):
                            last = pe.transpose(ps_src[0:EP, u * EP:(u + 1) * EP],
                                                key[:, q, 0, u:u + 1].to_broadcast([EP, EP]), ident[0:EP, 0:EP])
                        last.then_inc(turned_src, 1)

                    def before_silu(r, q):
                        g, s = r * Q4 + q, q % 2
                        pe.wait_ge(hotT_ready, g + 1)
                        pe.wait_ge(temb_ready, g + 1)
                        pe.wait_ge(q_loaded[q], (r + 1) * 16)
                        past(pe, pre_ready, g)
                        for u in range(U):
                            to = ps_pre[0:EP, u * H:(u + 1) * H]
                            pe.matmul(to, dst_hotT[:, s, u * EP:(u + 1) * EP], window_q[:, q, :],
                                      start=True, stop=False)
                            last = pe.matmul(to, ident[0:EP, 0:EP], temb[:, s, u, :], start=False, stop=True)
                        last.then_inc(q_ready, 1)

                    def count_pairs(r, q, chunks):
                        g, s = r * Q4 + q, q % 2
                        pe.wait_ge(pair_hot_ready, g + 1)
                        for c in chunks:
                            b, n = CHUNKS[c]
                            past(pe, pairs_used, g * NCH + (c - 1))
                            for u in range(U):
                                last = pe.matmul(ps_pair[(NCH * q + c) % 2][:, 0:n * WIN], src_hot[:, s, u, :],
                                                 pair_hot[:, s, u, b * WIN:(b + n) * WIN],
                                                 start=(u == 0), stop=(u == U - 1))
                            last.then_inc(pairs_ready, 1)

                    def sum_rows(r, q):
                        g, s = r * Q4 + q, q % 2
                        pe.wait_ge(hid_ready, g + 1)
                        pe.wait_ge(equal_ready, g + 1)
                        past(pe, sums_ready, g)
                        past(pe, dst_used, g)
                        for u in range(U):
                            pe.matmul(ps_sum[0:EP, u * H:(u + 1) * H], equal[:, s, u, :], hid[:, s, u, :],
                                      start=True, stop=True)
                        for u in range(U):
                            pe.matmul(ps_dst[:, 0:WIN], hid[:, s, u, :], dst_hot[:, s, u, :],
                                      start=(u == 0), stop=(u == U - 1))
                        for u in range(U):
                            pe.matmul(ps_dst[0:1, AT_CNT:AT_CNT + WIN], ones[:, :], dst_hot[:, s, u, :],
                                      start=(u == 0), stop=(u == U - 1))
                        for u in range(U):
                            last = pe.matmul(ps_dst[0:EP, AT_MULT + u:AT_MULT + u + 1], equal[:, s, u, :],
                                             ones[:, :], start=True, stop=True)
                        last.then_inc(summed, 1)

                    turn(0, 0)
                    before_silu(0, 0)

                    def work(r):
                        for q in range(Q4):
                            count_pairs(r, q, (0, 1))
                            if exists(r, q + 1):
                                turn(*after(r, q + 1))
                            count_pairs(r, q, (2,))
                            sum_rows(r, q)
                            if exists(r, q + 1):
                                before_silu(*after(r, q + 1))

                    rounds(pe, work, R)

        s_sb = sb("s_sb", [P, NT, W_ROW])

        def load_sums(sp, tables, done):
            full = (NT - 1) * P
            for u in range(U):
                sp.dma_start(tables[:, u, 0:NT - 1, :],
                             acc_src[u][0:full, :].rearrange("(t p) w -> p t w", p=P)).then_inc(done, 16)
                sp.dma_start(tables[0:REST, u, NT - 1, :], acc_src[u][full:N, :]).then_inc(done, 16)

        def join_tables(dve, tables):
            for u in range(1, U):
                chain(dve, dve.tensor_tensor(s_sb[:, :, :], (tables[:, 0] if u == 1 else s_sb)[:, :, :],
                                             tables[:, u, :, :], ALU.add))

        with ExitStack() as looking:
            tables = looking.enter_context(nc.sbuf_tensor("tables", [P, U, NT, W_ROW], F32))
            most = looking.enter_context(nc.sbuf_tensor("most", [P, 1], F32))
            tail_clear = looking.enter_context(nc.semaphore("tail_clear"))
            tables_loaded = looking.enter_context(nc.semaphore("tables_loaded"))
            most_ready = looking.enter_context(nc.semaphore("most_ready"))
            most_turned = looking.enter_context(nc.semaphore("most_turned"))

            with nc.Block() as block:
                @block.sync
                def _(sp):
                    sp.wait_ge(tail_clear, 1)
                    load_sums(sp, tables, tables_loaded)

                @block.vector
                def _(dve):
                    dve.memset(tables[:, :, NT - 1, :], 0.0).then_inc(tail_clear, 1)
                    dve.wait_ge(tables_loaded, 2 * U * 16)
                    join_tables(dve, tables)
                    dve.tensor_reduce(most[:, :], s_sb[:, :, H], AX_X, ALU.max).then_inc(most_ready, 1)
                    dve.wait_ge(most_turned, 1)
                    chain(dve, dve.tensor_reduce(flag[:, 1:2], psum[0][0:1, 0:P], AX_X, ALU.max))
                    dve.tensor_scalar(flag[:, 2:3], flag[:, 0:1], WIN - 0.5, None, ALU.is_gt)
                    chain(dve, dve.tensor_scalar(flag[:, 3:4], flag[:, 1:2], MAX_COUNT + 0.5, None, ALU.is_gt))
                    chain(dve, dve.tensor_tensor(flag_i[:, :], flag[:, 2:3], flag[:, 3:4], ALU.max))

                @block.tensor
                def _(pe):
                    pe.wait_ge(most_ready, 1)
                    pe.transpose(psum[0][0:1, 0:P], most[:, 0:1], ident[:, :]).then_inc(most_turned, 1)

        def if_general(eng):
            return eng.If(eng.value_load(flag_i[0:1, 0:1], min_val=0, max_val=1) == 1)

        with ExitStack() as gen:
            def gsb(name, shape, dt=F32):
                return gen.enter_context(nc.sbuf_tensor(name, shape, dt))

            def gsem(name):
                return gen.enter_context(nc.semaphore(name))

            g_zeros = gsb("g_zeros", [EP, N])
            g_wt = gsb("g_wt", [EP, H])
            g_bt = gsb("g_bt", [EP, H])
            g_lower = gsb("g_lower", [EP, EP])
            g_spare = gsb("g_spare", [EP, 3])
            g_key = gsb("g_key", [EP, 3, U])
            g_key_i = gsb("g_key_i", [EP, 2, U], I32)
            g_t = gsb("g_t", [EP, U])
            g_temb = gsb("g_temb", [EP, U, H])
            g_rows = gsb("g_rows", [EP, 2, U, H])
            g_equal = gsb("g_equal", [EP, 6, EP])
            g_counts = gsb("g_counts", [EP, 6, U])
            g_move = gsb("g_move", [EP, 3, U])
            g_to_row = gsb("g_to_row", [EP, 3, U], I32)
            g_hid = gsb("g_hid", [EP, U, H])
            g_sums = gsb("g_sums", [EP, 2, U, W_ROW])

            g_zeros_set = gsem("g_zeros_set")
            g_zeroed = gsem("g_zeroed")
            g_loaded = gsem("g_loaded")
            g_keys = gsem("g_keys")
            g_temb_in = gsem("g_temb_in")
            g_temb_out = gsem("g_temb_out")
            g_turned = gsem("g_turned")
            g_equal_ready = gsem("g_equal_ready")
            g_rows_ready = gsem("g_rows_ready")
            g_fetched = gsem("g_fetched")
            g_pre = gsem("g_pre")
            g_hid_ready = gsem("g_hid_ready")
            g_summed = gsem("g_summed")
            g_sums_ready = gsem("g_sums_ready")
            g_added = gsem("g_added")
            g_added_all = gsem("g_added_all")
            g_half = gsem("g_half")
            g_own = gsem("g_own")
            g_passed = gsem("g_passed")

            with nc.Block() as block:
                @block.sync
                def _(sp):
                    with if_general(sp):
                        for to, of in (
                            (g_wt[:, :], Wt.to_broadcast([EP, H])),
                            (g_bt[:, :], bt.rearrange("(o n) -> o n", o=1).to_broadcast([EP, H])),
                            (g_lower[:, :], below),
                            (g_spare[:, :], spare),
                        ):
                            sp.dma_start(to, of).then_inc(g_loaded, 16)
                        sp.wait_ge(g_zeros_set, 1)
                        n = 0
                        for k in range(N // EP):
                            sp.dma_start(pairs[k * EP * N:(k + 1) * EP * N, :].rearrange("(p c) o -> p (c o)", p=EP),
                                         g_zeros[:, :]).then_inc(g_zeroed, 16)
                            n += 1
                        for acc in [*acc_src, acc_dst]:
                            for k in range((N + EP) // EP):
                                sp.dma_start(acc[k * EP:(k + 1) * EP, :], g_zeros[:, 0:W_ROW]).then_inc(g_zeroed, 16)
                                n += 1
                        sp.dma_start(pairs[N * N:N * N + EP, :], g_zeros[:, 0:1]).then_inc(g_zeroed, 16)
                        sp.wait_ge(g_zeroed, 16 * (n + 1))

                @block.gpsimd
                def _(pool):
                    with if_general(pool):
                        pool.memset(g_zeros[:, :], 0.0).then_inc(g_zeros_set, 1)
                        pool.wait_ge(g_zeroed, 16 * (N // EP + (U + 1) * ((N + EP) // EP) + 1))
                        pool.sem_inc(g_added_all, 1)
                        with pool.Fori(0, G) as g:
                            pool.wait_ge(g_keys, g + 1)
                            pool.sem_inc(g_passed, 1)
                            for u in range(U):
                                for k, table in enumerate((table_p, table_q[0:N, :])):
                                    pool.indirect_dma_start(
                                        g_rows[:, k, u, :], None, table,
                                        bass.IndirectOffsetOnAxis(ap=g_key_i[:, k, u:u + 1], axis=0),
                                    ).then_inc(g_fetched, 16)
                            pool.wait_ge(g_rows_ready, g + 1)
                            pool.wait_ge(g_sums_ready, g + 1)
                            for u in range(U):
                                for k, (onto, rows_in) in enumerate((
                                    (acc_src[0], g_sums[:, 0, u, :]),
                                    (acc_dst, g_sums[:, 1, u, :]),
                                    (pairs, g_counts[:, 2, u:u + 1]),
                                )):
                                    pool.sem_inc(g_passed, 1)
                                    pool.indirect_dma_start(
                                        onto, bass.IndirectOffsetOnAxis(ap=g_to_row[:, k, u:u + 1], axis=0),
                                        rows_in, None, compute_op=ALU.add).then_inc(g_added, 16)
                                pool.wait_ge(g_added, (g * U + (u + 1)) * 48)
                            pool.sem_inc(g_added_all, 1)

                @block.vector
                def _(dve):
                    with if_general(dve):
                        dve.wait_ge(g_loaded, 64)
                        OWN_G = 2 + 3 * U + 2

                        with dve.Fori(0, G) as g:
                            def step(k, ins):
                                ins.then_inc(g_own, 1)
                                dve.wait_ge(g_own, g * OWN_G + k)

                            of = bass.ds(g * U, U)
                            dve.wait_ge(g_added_all, g + 1)
                            dve.tensor_copy(g_key[:, 0, :], edges[:, 0, of])
                            dve.tensor_copy(g_t[:, :], edges[:, 4, of])
                            step(1, dve.tensor_copy(g_key[:, 1, :], edges[:, 5, of]))
                            step(2, dve.scalar_tensor_tensor(g_key[:, 2, :], g_key[:, 0, :], float(N), g_key[:, 1, :],
                                                             ALU.mult, ALU.add))
                            dve.tensor_copy(g_key_i[:, :, :], g_key[:, 0:2, :]).then_inc(g_keys, 1)
                            for u in range(U):
                                last = dve.scalar_tensor_tensor(g_temb[:, u, :], g_wt[:, :], g_t[:, u:u + 1],
                                                                g_bt[:, :], ALU.mult, ALU.add)
                            last.then_inc(g_temb_in, 1)
                            dve.wait_ge(g_turned, g + 1)
                            for u in range(U):
                                if u >= 1:
                                    dve.wait_ge(g_summed, g * U + u)
                                for k in range(2):
                                    last = dve.tensor_scalar(g_equal[:, k, :], psum[k][0:EP, u * EP:(u + 1) * EP],
                                                             g_key[:, k, u:u + 1], None, ALU.is_equal)
                                last.then_inc(g_equal_ready, 1)
                                dve.wait_ge(g_equal_ready, g * U + (u + 1))
                                dve.tensor_tensor(g_equal[:, 2, :], g_equal[:, 0, :], g_equal[:, 1, :], ALU.mult)
                                step(3 + 3 * u, dve.tensor_tensor(
                                    g_equal[:, 3:5, :], g_equal[:, 0:2, :],
                                    g_lower[:, :].unsqueeze(1).to_broadcast([EP, 2, EP]), ALU.mult))
                                step(4 + 3 * u, dve.tensor_tensor(g_equal[:, 5, :], g_equal[:, 3, :],
                                                                  g_equal[:, 1, :], ALU.mult))
                                step(5 + 3 * u, dve.tensor_reduce(g_counts[:, :, u], g_equal[:, :, :], AX_X, ALU.add))
                                if u == 0:
                                    dve.wait_ge(g_fetched, (g + 1) * (2 * U * 16))
                                    dve.wait_ge(g_temb_out, g + 1)
                                    dve.tensor_tensor(g_rows[:, 0, :, :], g_rows[:, 0, :, :], g_rows[:, 1, :, :],
                                                      ALU.add).then_inc(g_half, 1)
                                    dve.wait_ge(g_half, g + 1)
                                    dve.tensor_tensor(g_rows[:, 0, :, :], g_rows[:, 0, :, :], g_temb[:, :, :],
                                                      ALU.add).then_inc(g_pre, 1)
                            n = 2 + 3 * U
                            step(n + 1, dve.tensor_tensor(g_move[:, :, :],
                                                          g_spare[:, :].unsqueeze(2).to_broadcast([EP, 3, U]),
                                                          g_key[:, :, :], ALU.subtract))
                            step(n + 2, dve.scalar_tensor_tensor(g_move[:, :, :], g_counts[:, 3:6, :], 0.5,
                                                                 g_move[:, :, :], ALU.is_gt, ALU.mult))
                            dve.tensor_tensor(g_to_row[:, :, :], g_move[:, :, :], g_key[:, :, :], ALU.add)
                            dve.tensor_copy(g_sums[:, :, :, H], g_counts[:, 0:2, :]).then_inc(g_rows_ready, 1)

                @block.scalar
                def _(act):
                    with if_general(act):
                        with act.Fori(0, G) as g:
                            act.wait_ge(g_temb_in, g + 1)
                            nc.scalar.activation(g_temb[:, :, :], g_temb[:, :, :], ACT.Silu).then_inc(g_temb_out, 1)
                            act.wait_ge(g_pre, g + 1)
                            nc.scalar.activation(g_hid[:, :, :], g_rows[:, 0, :, :], ACT.Silu).then_inc(g_hid_ready, 1)
                            act.wait_ge(g_summed, (g + 1) * U)
                            for k in range(2):
                                last = nc.scalar.copy(g_sums[:, k, :, 0:H],
                                                      psum[2 + k][0:EP, :].rearrange("p (u h) -> p u h", u=U))
                            last.then_inc(g_sums_ready, 1)

                @block.tensor
                def _(pe):
                    with if_general(pe):
                        with pe.Fori(0, G) as g:
                            pe.wait_ge(g_keys, g + 1)
                            for k in range(2):
                                for u in range(U):
                                    last = pe.transpose(psum[k][0:EP, u * EP:(u + 1) * EP],
                                                        g_key[:, k, u:u + 1].to_broadcast([EP, EP]),
                                                        ident[0:EP, 0:EP])
                            last.then_inc(g_turned, 1)
                            pe.wait_ge(g_hid_ready, g + 1)
                            for u in range(U):
                                pe.wait_ge(g_equal_ready, g * U + (u + 1))
                                for k in range(2):
                                    last = pe.matmul(psum[2 + k][0:EP, u * H:(u + 1) * H], g_equal[:, k, :],
                                                     g_hid[:, u, :], start=True, stop=True)
                                last.then_inc(g_summed, 1)

        with ExitStack() as turn_back:
            tables = turn_back.enter_context(nc.sbuf_tensor("tables_2", [P, U, NT, W_ROW], F32))
            by_dst = turn_back.enter_context(nc.sbuf_tensor("by_dst", [P, NT, W_ROW], F32))
            tail_clear_2 = turn_back.enter_context(nc.semaphore("tail_clear_2"))
            tables_loaded_2 = turn_back.enter_context(nc.semaphore("tables_loaded_2"))
            dst_turned = turn_back.enter_context(nc.semaphore("dst_turned"))
            joined = turn_back.enter_context(nc.semaphore("joined"))
            dst_taken = turn_back.enter_context(nc.semaphore("dst_taken"))

            with nc.Block() as block:
                @block.sync
                def _(sp):
                    with if_general(sp):
                        sp.wait_ge(tail_clear_2, 1)
                        load_sums(sp, tables, tables_loaded_2)
                        full = (NT - 1) * P
                        sp.dma_start(by_dst[:, 0:NT - 1, :], acc_dst[0:full, :].rearrange("(t p) w -> p t w", p=P))\
                            .then_inc(tables_loaded_2, 16)
                        sp.dma_start(by_dst[0:REST, NT - 1, :], acc_dst[full:N, :]).then_inc(tables_loaded_2, 16)

                @block.vector
                def _(dve):
                    with if_general(dve):
                        dve.memset(by_dst[:, NT - 1, :], 0.0)
                        dve.memset(tables[:, :, NT - 1, :], 0.0).then_inc(tail_clear_2, 1)
                        dve.wait_ge(tables_loaded_2, (2 * U + 2) * 16)
                        for u in range(1, U):
                            dve.tensor_tensor(s_sb[:, :, :], (tables[:, 0] if u == 1 else s_sb)[:, :, :],
                                              tables[:, u, :, :], ALU.add).then_inc(joined, 1)
                            dve.wait_ge(joined, u)
                        for t in range(NT):
                            n = rows(t)
                            dve.wait_ge(dst_turned, t + 1)
                            dve.tensor_copy(accT[:, t * P:t * P + n], psum[t % 2][:, 0:n])
                            dve.tensor_copy(cnt_row[:, t * P:t * P + n], psum[t % 2][0:1, P:P + n])\
                                .then_inc(dst_taken, 1)

                @block.tensor
                def _(pe):
                    with if_general(pe):
                        pe.wait_ge(tables_loaded_2, (2 * U + 2) * 16)
                        for t in range(NT):
                            if t >= 2:
                                pe.wait_ge(dst_taken, t - 1)
                            pe.transpose(psum[t % 2][:, 0:P], by_dst[:, t, 0:H], ident[:, :])
                            pe.transpose(psum[t % 2][0:1, P:2 * P], by_dst[:, t, H:H + 1], ident[:, :])\
                                .then_inc(dst_turned, 1)

        until_summed.close()

        x1 = sb("x1", [P, NT, D])
        hh = sb("hh", [P, NT, D])
        from_src = sb("from_src", [P, NT])
        nodes_summed = sem("nodes_summed")
        sT_ready = sem("sT_ready")
        sT_used = sem("sT_used")
        up_ready = sem("up_ready")
        up_used = sem("up_used")
        NP = NT * P
        CH = [(c, min(BANK, NP - c)) for c in range(0, NP, BANK)]
        late = ctx.enter_context(ExitStack())
        s2_row = sb("s2_row", [P, NP])

        with ExitStack() as back:
            def bsb(name, shape, dt=F32):
                return back.enter_context(nc.sbuf_tensor(name, shape, dt))

            h_sb = bsb("h2_sb", [P, NT, D])
            sT = bsb("sT", [P, 2, P])
            h2T = bsb("h2T", [D, NT, P])
            hhT = bsb("hhT", [D, NP])
            wT = bsb("wT", [D, D])
            a_col = bsb("a_col", [D, 1])
            a_rep = bsb("a_rep", [D, P])
            scored = bsb("scored", [P, NT, D])
            col_loaded = sem("col_loaded")
            rep_ready = sem("rep_ready")
            wT_ready = sem("wT_ready")
            wT_used = sem("wT_used")
            h2T_ready = sem("h2T_ready")
            h2T_used = sem("h2T_used")
            hh_ready = sem("hh_ready")
            hh_used = sem("hh_used")
            hhT_ready = sem("hhT_ready")
            hhT_used = sem("hhT_used")
            s2_ready = sem("s2_ready")
            s2_used = sem("s2_used")

            with nc.Block() as block:
                @block.sync
                def _(sp):
                    sp.dma_start(a_col[:, :], a[0:1, D:2 * D].rearrange("o d -> d o"),
                                 allow_slow_non_contiguous=True).then_inc(col_loaded, 16)

                @block.vector
                def _(dve):
                    chain(dve, dve.memset(x1[:, NT - 1, :], 0.0))
                    for t in range(NT):
                        n = rows(t)
                        dve.wait_ge(up_ready, t + 1)
                        dve.tensor_tensor(x1[0:n, t, :], psum[2 + t % 2][0:n, 0:D], x_sb[0:n, t, :],
                                          ALU.add).then_inc(up_used, 1)
                        dve.wait_ge(up_used, t + 1)
                        last = dve.scalar_tensor_tensor(x1[0:n, t, :], b2_row[0:n, 0:D], s_sb[0:n, t, H:H + 1],
                                                        x1[0:n, t, :], ALU.mult, ALU.add)
                    chain(dve, last)
                    layer_norm(dve, chain, x1, h_sb, 1)
                    dve.wait_ge(col_loaded, 16)
                    dve.tensor_copy(a_rep[:, :], a_col[:, 0:1].to_broadcast([D, P])).then_inc(rep_ready, 1)
                    dve.wait_ge(wT_ready, 1)
                    dve.tensor_copy(wT[:, :], psum[4][0:D, 0:D]).then_inc(wT_used, 1)
                    for t in range(NT):
                        dve.wait_ge(h2T_ready, t + 1)
                        dve.tensor_copy(h2T[:, t, :], psum[t % 2][0:D, 0:P]).then_inc(h2T_used, 1)
                    for t in range(NT):
                        dve.wait_ge(hh_ready, t + 1)
                        dve.tensor_copy(hh[:, t, :], psum[2 + t % 2][:, 0:D]).then_inc(hh_used, 1)
                    dve.wait_ge(hh_used, NT)
                    chain(dve, dve.tensor_tensor(scored[:, :, :], hh[:, :, :],
                                                 a_row[:, 0:D].unsqueeze(1).to_broadcast([P, NT, D]), ALU.mult))
                    chain(dve, dve.tensor_reduce(from_src[:, :], scored[:, :, :], AX_X, ALU.add))

                @block.scalar
                def _(act):
                    for t in range(NT):
                        act.wait_ge(sT_ready, t + 1)
                        if t >= 2:
                            act.wait_ge(up_ready, t - 1)
                        nc.scalar.copy(sT[:, t % 2, :], psum[t % 2][:, 0:P]).then_inc(sT_used, 1)
                    act.wait_ge(var_ready, 2)
                    nc.scalar.activation(std[:, :, :], mean_var[:, :, 1:2], ACT.Sqrt).then_inc(std_ready, 1)
                    for c, (lo, n) in enumerate(CH):
                        act.wait_ge(hhT_ready, c + 1)
                        nc.scalar.copy(hhT[:, lo:lo + n], psum[4 + c % 2][0:D, 0:n]).then_inc(hhT_used, 1)
                    for c, (lo, n) in enumerate(CH):
                        act.wait_ge(s2_ready, c + 1)
                        nc.scalar.copy(s2_row[:, lo:lo + n], psum[6 + c % 2][:, 0:n]).then_inc(s2_used, 1)

                @block.tensor
                def _(pe):
                    for t in range(NT + 1):
                        if t < NT:
                            if t >= 2:
                                pe.wait_ge(sT_used, t - 1)
                            pe.transpose(psum[t % 2][:, 0:P], s_sb[:, t, 0:H], ident[:, :]).then_inc(sT_ready, 1)
                        if t >= 1:
                            u = t - 1
                            pe.wait_ge(sT_used, u + 1)
                            if u >= 2:
                                pe.wait_ge(up_used, u - 1)
                            n = rows(u)
                            of = slice(u * P, u * P + n)
                            pe.matmul(psum[2 + u % 2][0:n, 0:D], sT[:, u % 2, 0:n], w2_sb[:, 0:D],
                                      start=True, stop=False)
                            pe.matmul(psum[2 + u % 2][0:n, 0:D], accT[:, of], w2_sb[:, D:2 * D],
                                      start=False, stop=False)
                            pe.matmul(psum[2 + u % 2][0:n, 0:D], cnt_row[:, of], b2_row[0:1, D:2 * D],
                                      start=False, stop=True).then_inc(up_ready, 1)
                    pe.transpose(psum[4][0:D, 0:D], w_sb[:, :], ident[0:D, 0:D]).then_inc(wT_ready, 1)
                    pe.wait_ge(h_ready, 2)
                    for t in range(NT):
                        if t >= 2:
                            pe.wait_ge(h2T_used, t - 1)
                        pe.transpose(psum[t % 2][0:D, 0:P], h_sb[:, t, :], ident[:, :]).then_inc(h2T_ready, 1)
                    pe.wait_ge(wT_used, 1)
                    pe.wait_ge(h2T_used, NT)
                    for t in range(NT):
                        if t >= 2:
                            pe.wait_ge(hh_used, t - 1)
                        pe.matmul(psum[2 + t % 2][:, 0:D], h2T[:, t, :], wT[:, :], start=True, stop=True)\
                            .then_inc(hh_ready, 1)
                    for c, (lo, n) in enumerate(CH):
                        if c >= 2:
                            pe.wait_ge(hhT_used, c - 1)
                        pe.matmul(psum[4 + c % 2][0:D, 0:n], wT[:, :],
                                  h2T[:, :, :].rearrange("d t p -> d (t p)")[:, lo:lo + n], start=True, stop=True)\
                            .then_inc(hhT_ready, 1)
                    pe.wait_ge(rep_ready, 1)
                    for c, (lo, n) in enumerate(CH):
                        pe.wait_ge(hhT_used, c + 1)
                        if c >= 2:
                            pe.wait_ge(s2_used, c - 1)
                        pe.matmul(psum[6 + c % 2][:, 0:n], a_rep[:, :], hhT[:, lo:lo + n], start=True, stop=True)\
                            .then_inc(s2_ready, 1)

        until_nodes.close()

        cnt = sb("cnt", [P, 2, N])
        score = sb("score", [P, 2, N])
        best = sb("best", [P, 2, 4])
        total = sb("total", [P, 2, 2])
        gain = sb("gain", [P, 2, D])
        low, act_out = cnt[0:D, 0, :], cnt[0:D, 1, :]
        y = sb("y", [P, NT, D])
        cnt_loaded = [sem("cnt_loaded_0"), sem("cnt_loaded_1")]
        best_ready = sem("best_ready")
        weights_ready = sem("weights_ready")
        gain_ready = sem("gain_ready")
        spread = sem("spread")
        low_ready = sem("low_ready")
        exp_ready = sem("exp_ready")
        elu_ready = sem("elu_ready")
        yT_ready = sem("yT_ready")
        y_ready = sem("y_ready")
        scored_all = sem("scored_all")
        lrelu_ready = sem("lrelu_ready")
        written = sem("written")
        general_way = sem("general_way")
        CN = [(lo, min(BANK, N - lo)) for lo in range(0, N, BANK)]
        assert len(CN) <= 7

        with nc.Block() as block:
            @block.sync
            def _(sp):
                with if_general(sp):
                    for t in range(NT):
                        n = rows(t)
                        if t >= 2:
                            sp.wait_ge(gain_ready, t - 1)
                        sp.dma_start(cnt[0:n, t % 2, :],
                                     pairs[t * P * N:(t * P + n) * N, :].rearrange("(p d) o -> p (d o)", p=n))\
                            .then_inc(cnt_loaded[t % 2], 16)
                    sp.wait_ge(cnt_loaded[0], 16 * ((NT + 1) // 2))
                    sp.wait_ge(cnt_loaded[1], 16 * (NT // 2))
                full = (NT - 1) * P
                sp.wait_ge(y_ready, NT)
                sp.dma_start(out[0:full, :].rearrange("(t p) d -> p t d", p=P), y[:, 0:NT - 1, :]).then_inc(written, 16)
                sp.dma_start(out[full:N, :], y[0:REST, NT - 1, :]).then_inc(written, 16)
                sp.wait_ge(written, 32)

            @block.gpsimd
            def _(pool):
                with if_general(pool):
                    pool.sem_inc(general_way, 1)
                with pool.Else():
                    for t in range(NT):
                        n = rows(t)
                        if t >= 2:
                            pool.wait_ge(gain_ready, t - 1)
                        pool.tensor_copy(cnt[0:n, t % 2, :], cols[0:n, t, 0:N]).then_inc(cnt_loaded[t % 2], 16)

            @block.vector
            def _(dve):
                def largest(t):
                    n, q = rows(t), t % 2
                    dve.wait_ge(cnt_loaded[q], 16 * (t // 2 + 1))
                    if t >= 2:
                        dve.wait_ge(spread, t - 1)
                    chain(dve, dve.tensor_scalar(score[0:n, q, :], cnt[0:n, q, :], 0.0, -FAR, ALU.is_equal, ALU.mult))
                    chain(dve, dve.tensor_tensor_reduce(score[0:n, q, :], score[0:n, q, :], s2_row[0:n, 0:N], 1.0,
                                                        -3.0 * FAR, ALU.add, ALU.max, best[0:n, q, 0:1]))
                    chain(dve, dve.tensor_tensor(best[0:n, q, 1:2], best[0:n, q, 0:1], from_src[0:n, t:t + 1], ALU.add))
                    chain(dve, dve.tensor_scalar(best[0:n, q, 2:3], best[0:n, q, 1:2], -SLOPE, None, ALU.mult))
                    dve.scalar_tensor_tensor(best[0:n, q, 3:4], best[0:n, q, 1:2], -1.0, best[0:n, q, 2:3],
                                             ALU.mult, ALU.min).then_inc(best_ready, 1)

                def leaky(t):
                    n, q = rows(t), t % 2
                    dve.wait_ge(scored_all, t + 1)
                    dve.scalar_tensor_tensor(score[0:n, q, :], score[0:n, q, :], SLOPE, score[0:n, q, :],
                                             ALU.mult, ALU.max).then_inc(lrelu_ready, 1)

                def weigh(t):
                    n, q = rows(t), t % 2
                    dve.wait_ge(weights_ready, t + 1)
                    chain(dve, dve.tensor_tensor_reduce(score[0:n, q, :], score[0:n, q, :], cnt[0:n, q, :], 1.0,
                                                        0.0, ALU.mult, ALU.add, total[0:n, q, 0:1]))
                    chain(dve, dve.tensor_scalar(total[0:n, q, 0:1], total[0:n, q, 0:1], 0.5, None, ALU.max))
                    chain(dve, dve.reciprocal(total[0:n, q, 1:2], total[0:n, q, 0:1]))
                    dve.tensor_scalar(gain[0:n, q, :], hh[0:n, t, :], total[0:n, q, 1:2], None,
                                      ALU.mult).then_inc(gain_ready, 1)

                largest(0)
                leaky(0)
                for t in range(NT):
                    if t + 1 < NT:
                        largest(t + 1)
                    weigh(t)
                    if t + 1 < NT:
                        leaky(t + 1)
                dve.wait_ge(spread, NT)
                for c, (lo, n) in enumerate(CN):
                    dve.tensor_scalar(low[:, lo:lo + n], psum[c][0:D, 0:n], 0.0, None, ALU.min).then_inc(low_ready, 1)
                for c, (lo, n) in enumerate(CN):
                    dve.wait_ge(exp_ready, c + 1)
                    chain(dve, dve.tensor_scalar(low[:, lo:lo + n], low[:, lo:lo + n], -1.0, None, ALU.add))
                    dve.scalar_tensor_tensor(act_out[:, lo:lo + n], psum[c][0:D, 0:n], 0.0, low[:, lo:lo + n],
                                             ALU.max, ALU.add).then_inc(elu_ready, 1)
                for t in range(NT):
                    dve.wait_ge(yT_ready, t + 1)
                    n = rows(t)
                    dve.tensor_tensor(y[0:n, t, :], psum[t % 2][0:n, 0:D], x1[0:n, t, :], ALU.add)\
                        .then_inc(y_ready, 1)

            @block.scalar
            def _(act):
                for t in range(NT):
                    n, q = rows(t), t % 2
                    act.wait_ge(best_ready, t + 1)
                    nc.scalar.activation(score[0:n, q, :], score[0:n, q, :], ACT.Identity,
                                         bias=from_src[0:n, t:t + 1]).then_inc(scored_all, 1)
                    act.wait_ge(lrelu_ready, t + 1)
                    nc.scalar.activation(score[0:n, q, :], score[0:n, q, :], ACT.Exp, bias=best[0:n, q, 3:4])\
                        .then_inc(weights_ready, 1)
                for c, (lo, n) in enumerate(CN):
                    act.wait_ge(low_ready, c + 1)
                    nc.scalar.activation(low[:, lo:lo + n], low[:, lo:lo + n], ACT.Exp).then_inc(exp_ready, 1)

            @block.tensor
            def _(pe):
                for t in range(NT):
                    n, q = rows(t), t % 2
                    pe.wait_ge(gain_ready, t + 1)
                    for c, (lo, m) in enumerate(CN):
                        last = pe.matmul(psum[c][0:D, 0:m], gain[0:n, q, :], score[0:n, q, lo:lo + m],
                                         start=(t == 0), stop=(t == NT - 1))
                    last.then_inc(spread, 1)
                pe.wait_ge(elu_ready, len(CN))
                for t in range(NT):
                    if t >= 2:
                        pe.wait_ge(y_ready, t - 1)
                    n = rows(t)
                    pe.transpose(psum[t % 2][0:n, 0:D], act_out[:, t * P:t * P + n], ident[0:D, 0:D])\
                        .then_inc(yT_ready, 1)


INPUTS = ["x", "src", "dst", "edge_weight", "L0_gnn_W1", "L0_gnn_b1", "L0_gnn_Wt", "L0_gnn_bt", "L0_gnn_W2",
          "L0_gnn_b2", "L1_gnn_W", "L1_gnn_a"]


def constants(N, E):
    rows = max(k for k in range(1, P + 1) if E % k == 0)
    p = np.arange(rows)
    return {
        "identity": np.eye(P, dtype=np.float32),
        "below": np.tril(np.ones((rows, rows), np.float32), -1),
        "spare": np.stack([N + p, N + p, N * N + p], 1).astype(np.float32),
        "steps": np.tile(np.arange((N + P - 1) // P * WIN, dtype=np.float16), (rows, 1)),
    }


def kernel(**inputs):
    import concourse.bacc as bacc
    from concourse.bass_utils import run_bass_kernel_spmd

    arrays = {name: np.ascontiguousarray(inputs[name]) for name in INPUTS}
    N, D = arrays["x"].shape
    arrays |= constants(N, arrays["src"].shape[0])
    nc = bacc.Bacc("TRN2", target_bir_lowering=False, num_devices=1)
    feeds, args = {}, []
    for name, value in arrays.items():
        feeds[f"in_{name}"] = value
        args.append(nc.dram_tensor(f"in_{name}", value.shape, mybir.dt.from_np(value.dtype), kind="ExternalInput").ap())
    args.append(nc.dram_tensor("out_x", (N, D), F32, kind="ExternalOutput").ap())
    build(nc, *args)
    got = run_bass_kernel_spmd(nc, [feeds], core_ids=[0])
    return got.results[0]["out_x"]
```
